# Optimizing a Trainium2 kernel written in Bass

```python
import numpy as np
import jax
import jax.numpy as jnp

def _softmax(x, axis=-1):
    return jax.nn.softmax(x, axis=axis)
def _gelu(x):
    return jax.nn.gelu(x, approximate=True)
def _silu(x):
    return jax.nn.silu(x)
def _sigmoid(x):
    return jax.nn.sigmoid(x)
def _layernorm(x, axis=-1, eps=1e-5):
    m = jnp.mean(x, axis=axis, keepdims=True)
    v = jnp.var(x, axis=axis, keepdims=True)
    return (x - m) / jnp.sqrt(v + eps)
def _scatter_add(tgt, idx, src, axis=0):
    return tgt.at[idx].add(src)
def _segment_sum(src, seg, n):
    return jax.ops.segment_sum(src, seg, n)

kernel_name = 'mk_conv_seq_d1_conv_nchw256_f40d03'

def setup_inputs(seed: int = 0):
    np.random.seed(seed)
    _w = jnp.asarray
    def _rec_inputs():
        import jax
        import jax.numpy as jnp
        _gk = jax.random.key(seed)
        x = 7.22e-05 + 1 * jax.random.normal(jax.random.fold_in(_gk, 1), (16, 256, 64, 32), jnp.float32)
        return x
    x = _rec_inputs()
    def _L0_conv_setup():
        import jax, jax.numpy as jnp
        import numpy as np
        B, C, H, W = (16, 256, 64, 32)
        HID = C // 8
        NEG = -9000000000000000.0

        def _spatial_adj(h, w):
            ii, jj = np.meshgrid(np.arange(h), np.arange(w), indexing='ij')
            pi, pj = (ii.reshape(-1), jj.reshape(-1))
            di = np.abs(pi[:, None] - pi[None, :])
            dj = np.abs(pj[:, None] - pj[None, :])
            return (di <= 1) & (dj <= 1) & ~((di == 0) & (dj == 0))

        def _channel_adj(c):
            i = np.arange(c)
            return np.abs(i[:, None] - i[None, :]) == 1

        def _bn_relu(y, g, b, m, v):
            inv = g / jnp.sqrt(v + 1e-05)
            return jax.nn.relu(y * inv[:, None, None] + (b - m * inv)[:, None, None])
        key = jax.random.key(seed)
        ks = jax.random.split(key, 12)
        return {'x': jax.random.normal(ks[0], (B, C, H, W), dtype=jnp.float32), 'wa': jax.random.normal(ks[1], (HID, C), dtype=jnp.float32) * 0.05, 'ga': jax.random.uniform(ks[2], (HID,), dtype=jnp.float32) + 0.5, 'ba': jax.random.normal(ks[3], (HID,), dtype=jnp.float32) * 0.1, 'ma': jnp.zeros((HID,), dtype=jnp.float32), 'va': jnp.ones((HID,), dtype=jnp.float32), 'ws': jax.random.normal(ks[4], (HID, C), dtype=jnp.float32) * 0.05, 'gs': jax.random.uniform(ks[5], (HID,), dtype=jnp.float32) + 0.5, 'bs': jax.random.normal(ks[6], (HID,), dtype=jnp.float32) * 0.1, 'ms': jnp.zeros((HID,), dtype=jnp.float32), 'vs': jnp.ones((HID,), dtype=jnp.float32), 'gama': jax.random.uniform(ks[7], (1,), dtype=jnp.float32)}
    _L0_conv_all = _L0_conv_setup()
    _L0_conv_in = {k: v for k, v in _L0_conv_all.items() if k in ('wa', 'ga', 'ba', 'ma', 'va', 'ws', 'gs', 'bs', 'ms', 'vs', 'gama', )}
    del _L0_conv_all

    return {
        "x": x,
        "L0_conv_wa": _L0_conv_in["wa"],
        "L0_conv_ga": _L0_conv_in["ga"],
        "L0_conv_ba": _L0_conv_in["ba"],
        "L0_conv_ma": _L0_conv_in["ma"],
        "L0_conv_va": _L0_conv_in["va"],
        "L0_conv_ws": _L0_conv_in["ws"],
        "L0_conv_gs": _L0_conv_in["gs"],
        "L0_conv_bs": _L0_conv_in["bs"],
        "L0_conv_ms": _L0_conv_in["ms"],
        "L0_conv_vs": _L0_conv_in["vs"],
        "L0_conv_gama": _L0_conv_in["gama"],
    }

def reference(x, L0_conv_wa, L0_conv_ga, L0_conv_ba, L0_conv_ma, L0_conv_va, L0_conv_ws, L0_conv_gs, L0_conv_bs, L0_conv_ms, L0_conv_vs, L0_conv_gama):
    import jax
    import jax.numpy as jnp
    def _L0_conv_ref(x, wa, ga, ba, ma, va, ws, gs, bs, ms, vs, gama):
        import jax, jax.numpy as jnp
        import numpy as np
        B, C, H, W = (16, 256, 64, 32)
        HID = C // 8
        NEG = -9000000000000000.0

        def _spatial_adj(h, w):
            ii, jj = np.meshgrid(np.arange(h), np.arange(w), indexing='ij')
            pi, pj = (ii.reshape(-1), jj.reshape(-1))
            di = np.abs(pi[:, None] - pi[None, :])
            dj = np.abs(pj[:, None] - pj[None, :])
            return (di <= 1) & (dj <= 1) & ~((di == 0) & (dj == 0))

        def _channel_adj(c):
            i = np.arange(c)
            return np.abs(i[:, None] - i[None, :]) == 1

        def _bn_relu(y, g, b, m, v):
            inv = g / jnp.sqrt(v + 1e-05)
            return jax.nn.relu(y * inv[:, None, None] + (b - m * inv)[:, None, None])
        b, c, h, w = x.shape
        n = h * w
        adj = jnp.asarray(_spatial_adj(h, w))
        cadj = jnp.asarray(_channel_adj(c))
        alpha = _bn_relu(jnp.einsum('bchw,oc->bohw', x, wa), ga, ba, ma, va)
        sigma = _bn_relu(jnp.einsum('bchw,oc->bohw', x, ws), gs, bs, ms, vs)
        xf = x.reshape(b, c, n)
        af = alpha.reshape(b, -1, n)
        sf = sigma.reshape(b, -1, n)
        att = jnp.einsum('bkn,bkm->bnm', af, sf)
        att = jax.nn.softmax(jnp.where(adj, att, NEG), axis=2)
        h_s = jnp.einsum('bnm,bcm->bcn', att, xf).reshape(b, c, h, w)
        Gc = jnp.einsum('bcn,bdn->bcd', xf, xf)
        catt = jax.nn.softmax(jnp.where(cadj, Gc, NEG), axis=2)
        h_p = jnp.einsum('bcd,bdn->bcn', catt, xf).reshape(b, c, h, w)
        h_prime = jax.nn.elu(h_s + h_p)
        return (1.0 - gama) * x + gama * h_prime

    def _gn(v, G=32, eps=1e-5):
        B_, C_, H_, W_ = v.shape
        g = v.reshape(B_, G, C_ // G, H_, W_)
        m = jnp.mean(g, axis=(2, 3, 4), keepdims=True)
        s = jnp.var(g, axis=(2, 3, 4), keepdims=True)
        return ((g - m) / jnp.sqrt(s + eps)).reshape(v.shape)

    def _ln_c(v, eps=1e-6):
        m = jnp.mean(v, axis=1, keepdims=True)
        s = jnp.var(v, axis=1, keepdims=True)
        return (v - m) / jnp.sqrt(s + eps)

    def _ln_t(v, eps=1e-5):
        m = jnp.mean(v, axis=-1, keepdims=True)
        s = jnp.var(v, axis=-1, keepdims=True)
        return (v - m) / jnp.sqrt(s + eps)

    def _to_tokens(v):
        B_, C_, H_, W_ = v.shape
        return v.reshape(B_, C_, H_ * W_).transpose(0, 2, 1)
    def _from_tokens(t, like):
        B_, C_, H_, W_ = like.shape
        return t.transpose(0, 2, 1).reshape(B_, C_, H_, W_)

    x = _L0_conv_ref(x, L0_conv_wa, L0_conv_ga, L0_conv_ba, L0_conv_ma, L0_conv_va, L0_conv_ws, L0_conv_gs, L0_conv_bs, L0_conv_ms, L0_conv_vs, L0_conv_gama)
    return x


_drawn_inputs = setup_inputs


def setup_inputs(seed=0):
    import zlib

    import numpy as np

    out = dict(_drawn_inputs(seed))
    spreads = {'L0_conv_ma': (0.0, 0.1),
     'L0_conv_va': (1.0, 0.6),
     'L0_conv_ms': (0.0, 0.3),
     'L0_conv_vs': (1.0, 0.594)}
    factors = {}
    for name, (base, spread) in spreads.items():
        noise = np.random.default_rng([zlib.crc32(name.encode()), seed]).standard_normal(out[name].shape)
        drawn = base * np.exp(spread * noise) if base else spread * noise
        out[name] = jnp.asarray(drawn.astype(out[name].dtype))
    for name, factor in factors.items():
        out[name] = (out[name] * factor).astype(out[name].dtype)
    return out
```

```python
from contextlib import ExitStack

import concourse.bass as bass
from concourse import mybir

B, C, H, W = 16, 256, 64, 32
HID = C // 8
P = 128
HALF = C // P
N = H * W
QUARTERS = P // HID
QR = H // QUARTERS
QN = QR * W
WR = 4
WIN = WR * W
NQ = WIN // 2
GROUPS = N // WIN
GQ = GROUPS // QUARTERS
BUFS = 3
FREE = 1
NEG = -9000000000000000.0
BAND = HID + 1
EVACS = GROUPS // 2 + 1

C_ID, C_DOWN, C_UP = 0, P, 2 * P
C_BAND = 3 * P
C_KEEP = C_BAND + 2 * BAND
C_END = C_KEEP + 4
C_MASK = C_END + 4
MASKS = 6 * WIN
C_ALL = C_MASK + MASKS


def graph_attention(nc, x, w_t, vectors, constants, out):
    fp32, bf16 = mybir.dt.float32, mybir.dt.bfloat16
    ALU = mybir.AluOpType
    ACT = mybir.ActivationFunctionType
    AX = mybir.AxisListType

    x_img = x.rearrange("b (p h) r w -> b p h (r w)", h=HALF)
    out_img = out.rearrange("b (p h) r w -> b p h (r w)", h=HALF)

    ctx = ExitStack()
    with ctx:
        def sb(name, shape, dt=fp32):
            return ctx.enter_context(nc.sbuf_tensor(name, shape, dt))

        def bank(name):
            return ctx.enter_context(nc.psum_tensor(name, [P, 512], fp32))

        def sem(name):
            return ctx.enter_context(nc.semaphore(name))

        xs = [sb(f"x{j}", [P, HALF, N + 2 * W]) for j in range(BUFS)]
        upper = sb("upper", [P, GROUPS + 1, C])
        lower = sb("lower", [P, GROUPS, C])
        const = sb("const", [P, C_ALL])
        ident_b = sb("ident_b", [P, P], bf16)
        mask_b = sb("mask_b", [P, MASKS], bf16)
        wt = sb("wt", [P, HALF, 2 * HID])
        vec = sb("vec", [P, 9])
        bn = sb("bn", [P, 8, 2])
        mix = sb("mix", [P, 1])
        query = sb("query", [P, QN])
        key = sb("key", [P, QN + 2 * W])
        neg_max = sb("neg_max", [P, QUARTERS, GQ])
        row_sum = sb("row_sum", [P, QUARTERS, GQ])
        row_inv = sb("row_inv", [P, QUARTERS, GQ])
        probs = [sb(f"probs{i}", [P, GQ, WIN]) for i in range(2)]
        probs_t = sb("probs_t", [P, QUARTERS, GQ * P])
        band = sb("band", [P, 2, 2, BAND])
        gram = sb("gram", [P, 2, 2])
        gram_k = sb("gram_k", [P, 2, 2])
        gram_e = sb("gram_e", [P, 2, 2])
        pair_max = sb("pair_max", [P, 2])
        gram_d = sb("gram_d", [P, 2, 2])
        gram_x = sb("gram_x", [P, 2, 2])
        pair_sum = sb("pair_sum", [P, 2])
        pair_inv = sb("pair_inv", [P, 2])
        catt = sb("catt", [P, 2, 2])
        mixer_part = sb("mixer_part", [P, 2, P])
        mixer = sb("mixer", [P, 2, P])
        mixer_t = sb("mixer_t", [P, 2 * P])
        elu = [sb(f"elu{h}", [P, QN]) for h in range(HALF)]
        blend = [sb(f"blend{i}", [P, HALF, QN]) for i in range(2)]

        xp = [bank("xp0"), bank("xp1")]
        pj = bank("pj")
        gb = bank("gb")
        et = bank("et")
        at = bank("at")
        z = [bank("z0"), bank("z1")]
        score = [at, z[0], z[1], at]

        const_in = sem("const_in")
        x_in = [sem(f"x_in{j}") for j in range(BUFS)]
        pads_done = sem("pads_done")
        casts_done = sem("casts_done")
        bn_step = sem("bn_step")
        bn_var = sem("bn_var")
        bn_root = sem("bn_root")
        bn_done = sem("bn_done")
        xt_done = sem("xt_done")
        xt_out = sem("xt_out")
        lower_in = [sem(f"lower_in{q}") for q in range(QUARTERS)]
        gram_done = sem("gram_done")
        proj_done = sem("proj_done")
        proj_out = sem("proj_out")
        score_done = sem("score_done")
        max_done = sem("max_done")
        exp_done = sem("exp_done")
        inv_done = sem("inv_done")
        probs_done = sem("probs_done")
        pt_done = sem("pt_done")
        pt_out = sem("pt_out")
        gram_step = sem("gram_step")
        gram_ready = sem("gram_ready")
        gram_exp = sem("gram_exp")
        mixer_done = sem("mixer_done")
        mt_done = sem("mt_done")
        mt_out = sem("mt_out")
        z_done = sem("z_done")
        ez_done = sem("ez_done")
        clip_done = sem("clip_done")
        elu_done = [sem(f"elu_done{h}") for h in range(HALF)]
        keep_done = sem("keep_done")
        blend_done = [sem(f"blend_done{h}") for h in range(HALF)]
        pool_passed = sem("pool_passed")
        stored = [sem(f"stored{i}") for i in range(2)]

        block = ctx.enter_context(nc.Block())
        ident = const[:, C_ID:C_ID + P]

        @block.sync
        def _(sp):
            def load_x(b, j):
                sp.dma_start(xs[j][:, :, W:W + N], x_img[b]).then_inc(x_in[j], 16)

            def build_lower(b, q):
                v0 = q * GQ
                sp.wait_ge(xt_out, EVACS * b + (EVACS if q == QUARTERS - 1 else 2 * (q + 1)))
                sp.dma_start(lower[0:64, v0:v0 + GQ, :], upper[64:128, v0:v0 + GQ, :]).then_inc(lower_in[q], 16)
                first, last = max(v0, 1), v0 + GQ + (q == QUARTERS - 1)
                sp.dma_start(lower[64:128, first - 1:last - 1, :], upper[0:64, first:last, :])\
                    .then_inc(lower_in[q], 16)

            def store(b, q):
                sp.wait_ge(blend_done[1], FREE + QUARTERS * b + q + 1)
                sp.wait_ge(blend_done[0], FREE + QUARTERS * b + q + 1)
                sp.dma_start(out_img[b, :, :, q * QN:(q + 1) * QN], blend[q % 2][:, :, :])\
                    .then_inc(stored[q % 2], 16)

            def image(b, j, load):
                for q in range(QUARTERS):
                    build_lower(b + 1, q)
                    store(b, q)
                if load:
                    load_x(b + BUFS, j)

            sp.dma_start(const[:, :], constants).then_inc(const_in, 16)
            sp.wait_ge(pads_done, BUFS * 2)
            load_x(0, 0)
            sp.dma_start(wt[:, :, :], w_t).then_inc(const_in, 16)
            sp.dma_start(vec[:, :], vectors).then_inc(const_in, 16)
            load_x(1, 1)
            load_x(2, 2)
            for q in range(QUARTERS):
                build_lower(0, q)
            with sp.Fori(0, B // BUFS - 1) as k:
                for j in range(BUFS):
                    image(k * BUFS + j, j, True)
            for b in range(B - B % BUFS - BUFS, B - 1):
                image(b, b % BUFS, b + BUFS < B)
            for q in range(QUARTERS):
                store(B - 1, q)
            for i in range(2):
                sp.wait_ge(stored[i], 16 * (FREE + B * QUARTERS // 2))

        @block.gpsimd
        def _(pool):
            def wait_apart(semaphore, count):
                pool.wait_ge(semaphore, count)
                pool.sem_inc(pool_passed, 1)

            def finish(b, j):
                for q in range(QUARTERS):
                    wait_apart(stored[q % 2], 16 * (FREE + 2 * b + q // 2))
                    if q == 0:
                        wait_apart(x_in[j], x_count(b, j))
                    nc.gpsimd.tensor_scalar(blend[q % 2][:, :, :], xs[j][:, :, W + q * QN:W + (q + 1) * QN],
                                            mix[:, 0:1], vec[:, 8:9], ALU.mult, ALU.subtract).then_inc(keep_done, 1)
                    for h in range(HALF):
                        wait_apart(ez_done, 2 * (QUARTERS * b + q) + h + 1)
                        nc.gpsimd.tensor_scalar(elu[h][:, :], elu[h][:, :], 1.0, None, ALU.min)\
                            .then_inc(clip_done, 1)

            def x_count(b, j):
                return 16 * (b // BUFS + 1) if isinstance(b, int) else 16 * (b_loop[0] + 1)

            b_loop = [None]
            for j in range(BUFS):
                nc.gpsimd.memset(xs[j][:, :, 0:W], 0.0).then_inc(pads_done, 1)
                nc.gpsimd.memset(xs[j][:, :, W + N:], 0.0).then_inc(pads_done, 1)
            for i in range(2):
                pool.sem_inc(stored[i], 16 * FREE)
            pool.wait_ge(bn_done, 1)
            with pool.Fori(0, B // BUFS) as k:
                b_loop[0] = k
                for j in range(BUFS):
                    finish(k * BUFS + j, j)
            finish(B - 1, (B - 1) % BUFS)

        @block.scalar
        def _(act):
            def move_xt(b, q):
                if q == QUARTERS - 1:
                    act.wait_ge(xt_done, EVACS * b + 2 * q + 1)
                    nc.scalar.activation(upper[0:64, GROUPS, :], pj[0:64, 0:C], ACT.Copy).then_inc(xt_out, 1)
                for t in range(2):
                    g = 2 * q + t
                    act.wait_ge(xt_done, EVACS * b + g + 1 + (q == QUARTERS - 1))
                    nc.scalar.activation(upper[:, 2 * g:2 * g + 2, :], xp[t][:, :].rearrange("p (v c) -> p v c", v=2),
                                         ACT.Copy).then_inc(xt_out, 1)

            def exp_z(b, q):
                for h in range(HALF):
                    act.wait_ge(z_done, 2 * (QUARTERS * b + q) + h + 1)
                    act.wait_ge(blend_done[h], FREE + QUARTERS * b + q)
                    nc.scalar.activation(elu[h][:, :], z[h][:, :], ACT.Exp).then_inc(ez_done, 1)

            def exp_scores(b, q):
                act.wait_ge(max_done, QUARTERS * b + q + 1)
                if not (isinstance(b, int) and b == 0 and q < 2):
                    act.wait_ge(pt_done, QUARTERS * b + q - 1)
                for v in range(GQ):
                    last = nc.scalar.activation(probs[q % 2][:, v, :], score[q][:, v * WIN:(v + 1) * WIN], ACT.Exp,
                                                bias=neg_max[:, q, v:v + 1], accum_out=row_sum[:, q, v:v + 1])
                last.then_inc(exp_done, 1)

            def attend(b):
                act.wait_ge(proj_done, 3 * b + 1)
                nc.scalar.activation(query[:, :], pj[:, :], ACT.Relu, bias=bn[:, 7, 0:1], scale=bn[:, 6, 0:1])\
                    .then_inc(proj_out, 1)
                act.wait_ge(proj_done, 3 * b + 2)
                nc.scalar.activation(key[:, W:W + QN], xp[0][:, :], ACT.Relu, bias=bn[:, 7, 1:2],
                                     scale=bn[:, 6, 1:2]).then_inc(proj_out, 1)
                act.wait_ge(proj_done, 3 * b + 3)
                nc.scalar.activation(key[:, :].rearrange("p (r w) -> p r w", w=W)[:, 0:QR + 2:QR + 1, :],
                                     xp[1][:, 0:2 * W].rearrange("p (r w) -> p r w", w=W), ACT.Relu,
                                     bias=bn[:, 7, 1:2], scale=bn[:, 6, 1:2]).then_inc(proj_out, 1)
                exp_scores(b, 0)
                act.wait_ge(gram_ready, b + 1)
                nc.scalar.activation(gram_x[:, :, :], gram_d[:, :, :], ACT.Exp).then_inc(gram_exp, 1)
                exp_scores(b, 1)
                exp_scores(b, 2)
                act.wait_ge(mt_done, b + 1)
                nc.scalar.activation(mixer_t[:, :], gb[:, 128:384], ACT.Copy).then_inc(mt_out, 1)
                exp_scores(b, 3)

            act.wait_ge(bn_var, 1)
            nc.scalar.activation(bn[:, 1, :], bn[:, 0, :], ACT.Sqrt).then_inc(bn_root, 1)
            act.wait_ge(bn_done, 1)
            for q in range(QUARTERS):
                move_xt(0, q)
            attend(0)
            with act.Fori(0, B // BUFS) as k:
                for j in range(BUFS):
                    b = k * BUFS + j
                    for q in range(QUARTERS):
                        exp_z(b, q)
                        move_xt(b + 1, q)
                    attend(b + 1)
            for q in range(QUARTERS):
                exp_z(B - 1, q)

        @block.vector
        def _(dve):
            steps = [0]

            def chain(ins):
                steps[0] += 1
                ins.then_inc(bn_step, 1)
                dve.wait_ge(bn_step, steps[0])

            def maxima(b, q):
                dve.wait_ge(score_done, QUARTERS * b + q + 1)
                nc.vector.reduce_max(neg_max[:, q, :], score[q][:, :].rearrange("p (v m) -> p v m", m=WIN), AX.X,
                                     negate=True).then_inc(max_done, 1)

            def normalise(b, q):
                dve.wait_ge(exp_done, QUARTERS * b + q + 1)
                nc.vector.reciprocal(row_inv[:, q, :], row_sum[:, q, :]).then_inc(inv_done, 1)
                dve.wait_ge(inv_done, QUARTERS * b + q + 1)
                nc.vector.tensor_tensor(probs[q % 2][:, :, :], probs[q % 2][:, :, :],
                                        row_inv[:, q, :].unsqueeze(2).to_broadcast([P, GQ, WIN]),
                                        ALU.mult).then_inc(probs_done, 1)

            def move_probs(b, q):
                dve.wait_ge(pt_done, QUARTERS * b + q + 1)
                nc.vector.tensor_copy(probs_t[:, q, :], et[:, :]).then_inc(pt_out, 1)

            def gram_softmax_in(b):
                def then(ins, n):
                    ins.then_inc(gram_step, 1)
                    dve.wait_ge(gram_step, GRAM_STEPS * b + n)
                dve.wait_ge(gram_done, b + 1)
                bands = gb[:, 0:2 * BAND].rearrange("p (s k) -> p s k", s=2)
                pick = const[:, C_BAND:C_BAND + 2 * BAND].rearrange("p (l k) -> p l k", l=2)
                for s in range(2):
                    last = nc.vector.tensor_tensor(band[:, s, :, :], pick,
                                                   bands[:, s, :].unsqueeze(1).to_broadcast([P, 2, BAND]), ALU.mult)
                then(last, 1)
                then(nc.vector.reduce_sum(gram[:, :, :], band[:, :, :, :], AX.X), 2)
                then(nc.vector.tensor_tensor(gram_k[:, :, :], gram[:, :, :],
                                             const[:, C_KEEP:C_KEEP + 4].rearrange("p (s l) -> p s l", s=2),
                                             ALU.mult), 3)
                then(nc.vector.tensor_tensor(gram_e[:, :, :], gram_k[:, :, :],
                                             const[:, C_END:C_END + 4].rearrange("p (s l) -> p s l", s=2),
                                             ALU.add), 4)
                then(nc.vector.reduce_max(pair_max[:, :], gram_e[:, :, :], AX.X), 5)
                nc.vector.tensor_tensor(gram_d[:, :, :], gram_e[:, :, :],
                                        pair_max[:, :].unsqueeze(2).to_broadcast([P, 2, 2]),
                                        ALU.subtract).then_inc(gram_ready, 1)

            def gram_softmax_out(b):
                def then(ins, n):
                    ins.then_inc(gram_step, 1)
                    dve.wait_ge(gram_step, GRAM_STEPS * b + n)
                dve.wait_ge(gram_exp, b + 1)
                then(nc.vector.reduce_sum(pair_sum[:, :], gram_x[:, :, :], AX.X), 6)
                then(nc.vector.reciprocal(pair_inv[:, :], pair_sum[:, :]), 7)
                then(nc.vector.tensor_tensor(catt[:, :, :], gram_x[:, :, :],
                                             pair_inv[:, :].unsqueeze(2).to_broadcast([P, 2, 2]), ALU.mult), 8)
                before = (const[:, C_DOWN:C_DOWN + P], ident)
                after = (ident, const[:, C_UP:C_UP + P])
                for s in range(2):
                    last = nc.vector.tensor_scalar(mixer_part[:, s, :], before[s], catt[:, s, 0:1], None, ALU.mult)
                then(last, 9)
                for s in range(2):
                    last = nc.vector.scalar_tensor_tensor(mixer[:, s, :], after[s], catt[:, s, 1:2],
                                                          mixer_part[:, s, :], ALU.mult, ALU.add)
                last.then_inc(mixer_done, 1)

            GRAM_STEPS = 9

            def attend(b):
                maxima(b, 0)
                maxima(b, 1)
                gram_softmax_in(b)
                maxima(b, 2)
                normalise(b, 0)
                gram_softmax_out(b)
                normalise(b, 1)
                move_probs(b, 0)
                maxima(b, 3)
                normalise(b, 2)
                move_probs(b, 1)
                normalise(b, 3)

            def finish(b):
                for q in range(QUARTERS):
                    for h in range(HALF):
                        dve.wait_ge(clip_done, 2 * (QUARTERS * b + q) + h + 1)
                        nc.vector.scalar_tensor_tensor(elu[h][:, :], z[h][:, :], 1.0, elu[h][:, :],
                                                       ALU.add, ALU.max).then_inc(elu_done[h], 1)
                    if q == 0:
                        move_probs(b, 2)
                    for h in range(HALF):
                        dve.wait_ge(keep_done, QUARTERS * b + q + 1)
                        dve.wait_ge(elu_done[h], QUARTERS * b + q + 1)
                        nc.vector.scalar_tensor_tensor(blend[q % 2][:, h, :], elu[h][:, :], vec[:, 8:9],
                                                       blend[q % 2][:, h, :], ALU.mult, ALU.add)\
                            .then_inc(blend_done[h], 1)
                    if q == 0:
                        move_probs(b, 3)

            dve.wait_ge(const_in, 48)
            nc.vector.tensor_copy(ident_b[:, :], ident).then_inc(casts_done, 1)
            nc.vector.tensor_copy(mask_b[:, :], const[:, C_MASK:C_MASK + MASKS]).then_inc(casts_done, 1)
            part = vec[:, 0:8].rearrange("p (s n) -> p n s", s=2)
            chain(nc.vector.tensor_scalar(bn[:, 0, :], part[:, 3, :], 1e-5, None, ALU.add))
            nc.vector.tensor_scalar(mix[:, :], vec[:, 8:9], -1.0, 1.0, ALU.mult, ALU.add).then_inc(bn_var, 1)
            dve.wait_ge(bn_root, 1)
            chain(nc.vector.reciprocal(bn[:, 2, :], bn[:, 1, :]))
            chain(nc.vector.tensor_tensor(bn[:, 3, :], bn[:, 0, :], bn[:, 2, :], ALU.mult))
            chain(nc.vector.tensor_tensor(bn[:, 4, :], bn[:, 1, :], bn[:, 3, :], ALU.add))
            chain(nc.vector.tensor_scalar(bn[:, 3, :], bn[:, 4, :], 0.5, None, ALU.mult))
            chain(nc.vector.reciprocal(bn[:, 5, :], bn[:, 3, :]))
            chain(nc.vector.tensor_tensor(bn[:, 6, :], part[:, 0, :], bn[:, 5, :], ALU.mult))
            chain(nc.vector.tensor_tensor(bn[:, 2, :], part[:, 2, :], bn[:, 6, :], ALU.mult))
            nc.vector.tensor_tensor(bn[:, 7, :], part[:, 1, :], bn[:, 2, :], ALU.subtract).then_inc(bn_done, 1)
            for h in range(HALF):
                dve.sem_inc(blend_done[h], FREE)
            attend(0)
            with dve.Fori(0, B // BUFS) as k:
                for j in range(BUFS):
                    b = k * BUFS + j
                    finish(b)
                    attend(b + 1)
            finish(B - 1)

        @block.tensor
        def _(pe):
            def mm(o, l, r, start, stop, **kw):
                return nc.tensor.matmul(o, l, r, start=start, stop=stop, skip_group_check=True, **kw)

            def transpose_x(b, j, q, first):
                xb = xs[j]
                if q == QUARTERS - 1:
                    for h in range(HALF):
                        last = nc.tensor.transpose(pj[0:64, h * P:(h + 1) * P], xb[:, h, GROUPS * WIN:GROUPS * WIN + 64],
                                                   ident)
                    last.then_inc(xt_done, 1)
                for t in range(2):
                    g = 2 * q + t
                    if q > 0:
                        pe.wait_ge(xt_out, EVACS * b + g - 1)
                    elif not first:
                        pe.wait_ge(proj_out, 3 * b - 1 + t)
                    for v in range(2):
                        for h in range(HALF):
                            at0 = (2 * g + v) * WIN
                            last = nc.tensor.transpose(xp[t][:, v * C + h * P:v * C + (h + 1) * P],
                                                       xb[:, h, at0:at0 + WIN], ident)
                    last.then_inc(xt_done, 1)

            def gram_band(b, q, first):
                last_q = q == QUARTERS - 1
                pe.wait_ge(xt_out, EVACS * b + (EVACS if last_q else 2 * (q + 1)))
                if q == 0 and not first:
                    pe.wait_ge(mt_out, b)
                for v in range(q * GQ, (q + 1) * GQ + last_q):
                    k = P if v < GROUPS else P // 2
                    for s in range(2):
                        for blk in range(P // HID):
                            mine = s * P + blk * HID
                            other = (1 - s) * P + blk * HID - (1 - s)
                            last = mm(gb[blk * HID:(blk + 1) * HID, s * BAND:(s + 1) * BAND],
                                      upper[0:k, v, mine:mine + HID], upper[0:k, v, other:other + BAND],
                                      v == 0 and s == 0, v == GROUPS, tile_position=(0, blk * HID))
                if last_q:
                    last.then_inc(gram_done, 1)

            def project(b, j):
                xb = xs[j]
                pe.wait_ge(xt_out, EVACS * b + 2 * QUARTERS - 1)
                for h in range(HALF):
                    for q in range(QUARTERS):
                        last = mm(pj[q * HID:(q + 1) * HID, :], wt[:, h, 0:HID], xb[:, h, W + q * QN:W + (q + 1) * QN],
                                  h == 0, h == HALF - 1, tile_position=(0, q * HID))
                last.then_inc(proj_done, 1)
                pe.wait_ge(xt_out, EVACS * b + EVACS)
                for h in range(HALF):
                    for q in range(QUARTERS):
                        last = mm(xp[0][q * HID:(q + 1) * HID, :], wt[:, h, HID:], xb[:, h, W + q * QN:W + (q + 1) * QN],
                                  h == 0, h == HALF - 1, tile_position=(0, q * HID))
                last.then_inc(proj_done, 1)
                for h in range(HALF):
                    rows = xb[:, h, :].rearrange("p (r w) -> p r w", w=W)
                    for q in range(QUARTERS):
                        last = mm(xp[1][q * HID:(q + 1) * HID, 0:2 * W], wt[:, h, HID:],
                                  rows[:, q * QR:q * QR + QR + 2:QR + 1, :],
                                  h == 0, h == HALF - 1, tile_position=(0, q * HID))
                last.then_inc(proj_done, 1)

            def scores(b, q, first):
                if q == 0:
                    pe.wait_ge(proj_out, 3 * b + 3)
                    if not first:
                        pe.wait_ge(exp_done, QUARTERS * b)
                elif q < 3:
                    if not first:
                        pe.wait_ge(elu_done[q - 1], QUARTERS * b)
                else:
                    pe.wait_ge(exp_done, QUARTERS * b + 1)
                m0 = (q > 0) * WIN + (q == QUARTERS - 1) * WIN
                mm(score[q][:, :], ident_b[:, :], mask_b[:, m0:m0 + GQ * WIN], True, False)
                lo = q * HID
                for v in range(GQ):
                    for c in range(2):
                        last = mm(score[q][c * 64:(c + 1) * 64, v * WIN:(v + 1) * WIN],
                                  query[lo:lo + HID, v * WIN + c * NQ:v * WIN + (c + 1) * NQ],
                                  key[lo:lo + HID, v * WIN + c * 2 * W:v * WIN + c * 2 * W + WIN],
                                  False, True, tile_position=(lo, c * 64))
                last.then_inc(score_done, 1)

            def transpose_probs(b, q, first):
                pe.wait_ge(probs_done, QUARTERS * b + q + 1)
                if not (first and q == 0):
                    pe.wait_ge(pt_out, QUARTERS * b + q)
                for v in range(GQ):
                    last = nc.tensor.transpose(et[:, v * P:(v + 1) * P], probs[q % 2][:, v, :], ident)
                last.then_inc(pt_done, 1)

            def transpose_mixer(b):
                pe.wait_ge(mixer_done, b + 1)
                for s in range(2):
                    last = nc.tensor.transpose(gb[:, (1 + s) * P:(2 + s) * P], mixer[:, s, :], ident)
                last.then_inc(mt_done, 1)

            def attend(b, j, first=False):
                project(b, j)
                gram_band(b, 3, first)
                for q in range(3):
                    scores(b, q, first)
                transpose_probs(b, 0, first)
                transpose_mixer(b)
                scores(b, 3, first)
                transpose_probs(b, 1, first)

            def combine(b, j, q):
                xb = xs[j]
                if q == 0:
                    pe.wait_ge(mt_out, b + 1)
                pe.wait_ge(pt_out, QUARTERS * b + q + 1)
                pe.wait_ge(lower_in[q], 32 * (b + 1))
                if q + 1 < QUARTERS:
                    pe.wait_ge(lower_in[q + 1], 32 * (b + 1))
                for h in range(HALF):
                    if q == 0:
                        pe.wait_ge(exp_done, QUARTERS * b + h + 2)
                    else:
                        pe.wait_ge(elu_done[h], QUARTERS * b + q)
                    mm(z[h][:, :], mixer_t[:, h * P:(h + 1) * P], xb[:, 1 - h, W + q * QN:W + (q + 1) * QN],
                       True, False)
                    for v in range(GQ):
                        for c, window in enumerate((upper, lower)):
                            col = v * P + c * NQ
                            last = mm(z[h][:, col:col + NQ], window[:, q * GQ + v, h * P:(h + 1) * P],
                                      probs_t[:, q, col:col + NQ], False, v == GQ - 1 and c == 1)
                    last.then_inc(z_done, 1)

            pe.wait_ge(const_in, 48)
            pe.wait_ge(casts_done, 2)
            pe.wait_ge(x_in[0], 16)
            for q in range(QUARTERS):
                transpose_x(0, 0, q, True)
                if q < QUARTERS - 1:
                    gram_band(0, q, True)
            attend(0, 0, True)
            with pe.Fori(0, B // BUFS) as k:
                for j in range(BUFS):
                    b = k * BUFS + j
                    n = (j + 1) % BUFS
                    combine(b, j, 0)
                    transpose_probs(b, 2, False)
                    pe.wait_ge(x_in[n], 16 * (k + 1 + (j + 1) // BUFS))
                    transpose_x(b + 1, n, 0, False)
                    transpose_probs(b, 3, False)
                    combine(b, j, 1)
                    gram_band(b + 1, 0, False)
                    transpose_x(b + 1, n, 1, False)
                    combine(b, j, 2)
                    gram_band(b + 1, 1, False)
                    transpose_x(b + 1, n, 2, False)
                    combine(b, j, 3)
                    gram_band(b + 1, 2, False)
                    transpose_x(b + 1, n, 3, False)
                    attend(b + 1, n)
            last = (B - 1) % BUFS
            combine(B - 1, last, 0)
            transpose_probs(B - 1, 2, False)
            combine(B - 1, last, 1)
            transpose_probs(B - 1, 3, False)
            combine(B - 1, last, 2)
            combine(B - 1, last, 3)


def shape_constants():
    import numpy as np
    const = np.zeros((P, C_ALL), np.float32)
    i = np.arange(P)
    const[i, C_ID + i] = 1.0
    const[i[1:], C_DOWN + i[:-1]] = 1.0
    const[i[:-1], C_UP + i[1:]] = 1.0
    const[i, C_BAND + i % HID] = 1.0
    const[i, C_BAND + BAND + i % HID + 1] = 1.0
    const[:, C_KEEP:C_KEEP + 4] = 1.0
    const[0, C_KEEP] = 0.0
    const[P - 1, C_KEEP + 3] = 0.0
    const[0, C_END] = NEG
    const[P - 1, C_END + 3] = NEG
    kind, query_row, query_col = i // NQ, (i // W) % 2 + 1, i % W
    key_row, key_col = np.arange(WIN) // W, np.arange(WIN) % W
    di = abs(query_row[:, None] - key_row)
    dj = abs(query_col[:, None] - key_col)
    near = (di <= 1) & (dj <= 1) & ~((di == 0) & (dj == 0))
    for n in range(6):
        inside = np.ones((P, WIN), bool)
        if n == 0:
            inside &= ~((kind[:, None] == 0) & (key_row == 0))
        if n == 5:
            inside &= ~((kind[:, None] == 1) & (key_row == WR - 1))
        const[:, C_MASK + n * WIN:C_MASK + (n + 1) * WIN] = np.where(near & inside, 0.0, NEG)
    return const


def kernel(**inputs):
    import numpy as np
    import concourse.bacc as bacc
    from concourse.bass_utils import run_bass_kernel_spmd

    a = {name.replace("L0_conv_", ""): np.asarray(v) for name, v in inputs.items()}
    w_t = np.concatenate([a["wa"], a["ws"]], axis=0).T.reshape(P, HALF, 2 * HID)
    norms = np.stack([a[n + s] for s in "as" for n in "gbmv"], axis=1)
    vectors = np.concatenate([np.tile(norms, (QUARTERS, 1)), np.tile(a["gama"].reshape(1, 1), (P, 1))], axis=1)
    arrays = {"x_dram": a["x"], "w_dram": w_t, "vectors_dram": vectors, "constants_dram": shape_constants()}
    arrays = {name: np.ascontiguousarray(v) for name, v in arrays.items()}

    nc = bacc.Bacc("TRN2", target_bir_lowering=False, num_devices=1)
    args = [nc.dram_tensor(name, v.shape, mybir.dt.from_np(v.dtype), kind="ExternalInput").ap()
            for name, v in arrays.items()]
    out = nc.dram_tensor("out_dram", (B, C, H, W), mybir.dt.float32, kind="ExternalOutput").ap()
    graph_attention(nc, *args, out)
    result = run_bass_kernel_spmd(nc, [arrays], core_ids=[0])
    return result.results[0]["out_dram"]
```

```python
from contextlib import ExitStack

import concourse.bass as bass
from concourse import mybir

B, C, H, W = 16, 256, 64, 32
HID = C // 8
P = 128
HALF = C // P
N = H * W
QUARTERS = P // HID
QR = H // QUARTERS
QN = QR * W
WR = 4
WIN = WR * W
NQ = WIN // 2
GROUPS = N // WIN
GQ = GROUPS // QUARTERS
BUFS = 3
FREE = 1
NEG = -9000000000000000.0
BAND = HID + 1
EVACS = GROUPS // 2 + 1
PARTS = 2
GV = GQ // PARTS
SUMS = PARTS * QUARTERS
SHIFT = 400

C_ID, C_DOWN, C_UP = 0, P, 2 * P
C_BAND = 3 * P
C_END = C_BAND + 3 * BAND
C_MASK = C_END + 4
MASKS = 6 * WIN
C_ALL = C_MASK + MASKS


def graph_attention(nc, x, w_t, vectors, constants, out):
    fp32, bf16 = mybir.dt.float32, mybir.dt.bfloat16
    ALU = mybir.AluOpType
    ACT = mybir.ActivationFunctionType
    AX = mybir.AxisListType

    x_img = x.rearrange("b (p h) r w -> b p h (r w)", h=HALF)
    out_img = out.rearrange("b (p h) r w -> b p h (r w)", h=HALF)

    ctx = ExitStack()
    with ctx:
        def sb(name, shape, dt=fp32):
            return ctx.enter_context(nc.sbuf_tensor(name, shape, dt))

        def bank(name):
            return ctx.enter_context(nc.psum_tensor(name, [P, 512], fp32))

        def sem(name):
            return ctx.enter_context(nc.semaphore(name))

        xs = [sb(f"x{j}", [P, HALF, N + 2 * W]) for j in range(BUFS)]
        upper = sb("upper", [P, GROUPS + 1, C])
        lower = sb("lower", [P, GROUPS, C])
        const = sb("const", [P, C_ALL])
        ident_b = sb("ident_b", [P, P], bf16)
        mask_b = sb("mask_b", [P, MASKS], bf16)
        wt = sb("wt", [P, HALF, 2 * HID])
        vec = sb("vec", [P, 9])
        bn = sb("bn", [P, 8, 2])
        mix = sb("mix", [P, 2])
        query = sb("query", [P, QN])
        key = sb("key", [P, QN + 2 * W])
        neg_max = sb("neg_max", [P, QUARTERS, GQ])
        row_sum = sb("row_sum", [P, QUARTERS, GQ])
        row_inv = sb("row_inv", [P, QUARTERS, GQ])
        probs = [sb(f"probs{i}", [P, GQ, WIN]) for i in range(2)]
        probs_t = sb("probs_t", [P, QUARTERS, GQ * P])
        spatial = sb("spatial", [P, GQ, C])
        band = sb("band", [P, 3, BAND])
        gram = sb("gram", [P, 3])
        gram_e = sb("gram_e", [P, 2, 2])
        pair_max = sb("pair_max", [P, 2])
        gram_d = sb("gram_d", [P, 2, 2])
        gram_x = sb("gram_x", [P, 2, 2])
        pair_sum = sb("pair_sum", [P, 2])
        pair_inv = sb("pair_inv", [P, 2])
        catt = sb("catt", [P, 2, 2])
        mixer_part = sb("mixer_part", [P, 2, P])
        mixer = sb("mixer", [P, 2, P])
        mixer_t = sb("mixer_t", [P, 2 * P])
        elu = [sb(f"elu{h}", [P, QN]) for h in range(HALF)]
        blend = [sb(f"blend{i}", [P, HALF, QN]) for i in range(2)]

        xp = [bank("xp0"), bank("xp1")]
        pj = bank("pj")
        gb = bank("gb")
        et = bank("et")
        at = bank("at")
        z = [bank("z0"), bank("z1")]
        score = [at, z[0], z[1], at]
        part_bank = [pj, at]

        const_in = sem("const_in")
        x_in = [sem(f"x_in{j}") for j in range(BUFS)]
        pads_done = sem("pads_done")
        casts_done = sem("casts_done")
        bn_step = sem("bn_step")
        bn_var = sem("bn_var")
        bn_root = sem("bn_root")
        bn_done = sem("bn_done")
        xt_done = sem("xt_done")
        xt_out = sem("xt_out")
        lower_in = [sem(f"lower_in{q}") for q in range(QUARTERS)]
        gram_done = sem("gram_done")
        proj_done = sem("proj_done")
        proj_out = sem("proj_out")
        score_done = sem("score_done")
        max_done = sem("max_done")
        exp_done = sem("exp_done")
        inv_done = sem("inv_done")
        pt_done = sem("pt_done")
        pt_out = sem("pt_out")
        hs_done = sem("hs_done")
        hs_out = sem("hs_out")
        gram_step = sem("gram_step")
        gram_side = sem("gram_side")
        shift_done = sem("shift_done")
        gram_ready = sem("gram_ready")
        gram_exp = sem("gram_exp")
        mixer_done = sem("mixer_done")
        mt_done = sem("mt_done")
        mt_out = sem("mt_out")
        z_done = sem("z_done")
        ez_done = sem("ez_done")
        clip_done = sem("clip_done")
        elu_done = [sem(f"elu_done{h}") for h in range(HALF)]
        keep_done = sem("keep_done")
        blend_done = [sem(f"blend_done{h}") for h in range(HALF)]
        stored = [sem(f"stored{i}") for i in range(2)]

        block = ctx.enter_context(nc.Block())
        ident = const[:, C_ID:C_ID + P]

        @block.sync
        def _(sp):
            def load_x(b, j):
                sp.dma_start(xs[j][:, :, W:W + N], x_img[b]).then_inc(x_in[j], 16)

            def build_lower(b, q):
                v0 = q * GQ
                sp.wait_ge(xt_out, EVACS * b + (EVACS if q == QUARTERS - 1 else 2 * (q + 1)))
                sp.dma_start(lower[0:64, v0:v0 + GQ, :], upper[64:128, v0:v0 + GQ, :]).then_inc(lower_in[q], 16)
                first, last = max(v0, 1), v0 + GQ + (q == QUARTERS - 1)
                sp.dma_start(lower[64:128, first - 1:last - 1, :], upper[0:64, first:last, :])\
                    .then_inc(lower_in[q], 16)

            def store(b, q):
                sp.wait_ge(blend_done[1], FREE + QUARTERS * b + q + 1)
                sp.wait_ge(blend_done[0], FREE + QUARTERS * b + q + 1)
                sp.dma_start(out_img[b, :, :, q * QN:(q + 1) * QN], blend[q % 2][:, :, :])\
                    .then_inc(stored[q % 2], 16)

            def image(b, j, load):
                for q in range(QUARTERS):
                    build_lower(b + 1, q)
                    store(b, q)
                if load:
                    load_x(b + BUFS, j)

            sp.dma_start(const[:, :], constants).then_inc(const_in, 16)
            sp.wait_ge(pads_done, BUFS * 2)
            load_x(0, 0)
            sp.dma_start(wt[:, :, :], w_t).then_inc(const_in, 16)
            sp.dma_start(vec[:, :], vectors).then_inc(const_in, 16)
            load_x(1, 1)
            load_x(2, 2)
            for q in range(QUARTERS):
                build_lower(0, q)
            with sp.Fori(0, B // BUFS - 1) as k:
                for j in range(BUFS):
                    image(k * BUFS + j, j, True)
            for b in range(B - B % BUFS - BUFS, B - 1):
                image(b, b % BUFS, b + BUFS < B)
            for q in range(QUARTERS):
                store(B - 1, q)
            for i in range(2):
                sp.wait_ge(stored[i], 16 * (FREE + B * QUARTERS // 2))

        @block.gpsimd
        def _(pool):
            for j in range(BUFS):
                nc.gpsimd.memset(xs[j][:, :, 0:W], 0.0).then_inc(pads_done, 1)
                nc.gpsimd.memset(xs[j][:, :, W + N:], 0.0).then_inc(pads_done, 1)
            for i in range(2):
                pool.sem_inc(stored[i], 16 * FREE)

        @block.scalar
        def _(act):
            def move_xt(b, q):
                for t in range(2):
                    g = 2 * q + t
                    act.wait_ge(xt_done, EVACS * b + g + 1 + (g == EVACS - 2))
                    nc.scalar.activation(upper[:, 2 * g:2 * g + 2, :], xp[t][:, :].rearrange("p (v c) -> p v c", v=2),
                                         ACT.Copy).then_inc(xt_out, 1)
                    if g == EVACS - 3:
                        act.wait_ge(xt_done, EVACS * b + g + 2)
                        nc.scalar.activation(upper[0:64, GROUPS, :], et[0:64, 0:C], ACT.Copy).then_inc(xt_out, 1)

            def exp_z(b, q):
                for h in range(HALF):
                    act.wait_ge(z_done, 2 * (QUARTERS * b + q) + h + 1)
                    act.wait_ge(blend_done[h], FREE + QUARTERS * b + q)
                    nc.scalar.activation(elu[h][:, :], z[h][:, :], ACT.Exp).then_inc(ez_done, 1)

            def keep_x(b, j, q):
                act.wait_ge(stored[q % 2], 16 * (FREE + 2 * b + q // 2))
                nc.scalar.activation(blend[q % 2][:, :, :], xs[j][:, :, W + q * QN:W + (q + 1) * QN], ACT.Identity,
                                     bias=mix[:, 1:2], scale=mix[:, 0:1]).then_inc(keep_done, 1)

            def exp_scores(b, q):
                act.wait_ge(max_done, QUARTERS * b + q + 1)
                if not (isinstance(b, int) and b == 0 and q < 2):
                    act.wait_ge(pt_done, QUARTERS * b + q - 1)
                for v in range(GQ):
                    last = nc.scalar.activation(probs[q % 2][:, v, :], score[q][:, v * WIN:(v + 1) * WIN], ACT.Exp,
                                                bias=neg_max[:, q, v:v + 1], accum_out=row_sum[:, q, v:v + 1])
                last.then_inc(exp_done, 1)

            def move_probs(b, q):
                act.wait_ge(pt_done, QUARTERS * b + q + 1)
                nc.scalar.activation(probs_t[:, q, :], et[:, :], ACT.Copy).then_inc(pt_out, 1)

            def attend(b):
                act.wait_ge(proj_done, 3 * b + 1)
                nc.scalar.activation(query[:, :], pj[:, :], ACT.Relu, bias=bn[:, 7, 0:1], scale=bn[:, 6, 0:1])\
                    .then_inc(proj_out, 1)
                act.wait_ge(proj_done, 3 * b + 2)
                nc.scalar.activation(key[:, W:W + QN], xp[0][:, :], ACT.Relu, bias=bn[:, 7, 1:2],
                                     scale=bn[:, 6, 1:2]).then_inc(proj_out, 1)
                act.wait_ge(proj_done, 3 * b + 3)
                nc.scalar.activation(key[:, :].rearrange("p (r w) -> p r w", w=W)[:, 0:QR + 2:QR + 1, :],
                                     xp[1][:, 0:2 * W].rearrange("p (r w) -> p r w", w=W), ACT.Relu,
                                     bias=bn[:, 7, 1:2], scale=bn[:, 6, 1:2]).then_inc(proj_out, 1)
                exp_scores(b, 0)
                act.wait_ge(gram_ready, b + 1)
                nc.scalar.activation(gram_x[:, :, :], gram_d[:, :, :], ACT.Exp).then_inc(gram_exp, 1)
                exp_scores(b, 1)
                move_probs(b, 0)
                exp_scores(b, 2)
                act.wait_ge(mt_done, b + 1)
                nc.scalar.activation(mixer_t[:, :], gb[:, P:3 * P], ACT.Copy).then_inc(mt_out, 1)
                move_probs(b, 1)
                exp_scores(b, 3)

            act.wait_ge(bn_var, 1)
            nc.scalar.activation(bn[:, 1, :], bn[:, 0, :], ACT.Sqrt).then_inc(bn_root, 1)
            act.wait_ge(bn_done, 1)
            for q in range(QUARTERS):
                move_xt(0, q)
            attend(0)
            with act.Fori(0, B // BUFS) as k:
                for j in range(BUFS):
                    b = k * BUFS + j
                    act.wait_ge(x_in[j], 16 * (k + 1))
                    move_probs(b, 2)
                    keep_x(b, j, 0)
                    move_probs(b, 3)
                    for q in range(QUARTERS):
                        exp_z(b, q)
                        move_xt(b + 1, q)
                        if q + 1 < QUARTERS:
                            keep_x(b, j, q + 1)
                    attend(b + 1)
            last = (B - 1) % BUFS
            act.wait_ge(x_in[last], 16 * ((B - 1) // BUFS + 1))
            move_probs(B - 1, 2)
            keep_x(B - 1, last, 0)
            move_probs(B - 1, 3)
            for q in range(QUARTERS):
                exp_z(B - 1, q)
                if q + 1 < QUARTERS:
                    keep_x(B - 1, last, q + 1)

        @block.vector
        def _(dve):
            steps = [0]

            def chain(ins):
                steps[0] += 1
                ins.then_inc(bn_step, 1)
                dve.wait_ge(bn_step, steps[0])

            def maxima(b, q):
                dve.wait_ge(score_done, QUARTERS * b + q + 1)
                nc.vector.reduce_max(neg_max[:, q, :], score[q][:, :].rearrange("p (v m) -> p v m", m=WIN), AX.X,
                                     negate=True).then_inc(max_done, 1)

            def weigh(b, q):
                for t in range(PARTS):
                    dve.wait_ge(hs_done, SUMS * b + PARTS * q + t + 1)
                    nc.vector.tensor_tensor(spatial[:, t * GV:(t + 1) * GV, :],
                                            part_bank[t][:, :].rearrange("p (v c) -> p v c", v=GV),
                                            row_inv[:, q, t * GV:(t + 1) * GV].unsqueeze(2).to_broadcast([P, GV, C]),
                                            ALU.mult).then_inc(hs_out, 1)

            def gram_pick(b):
                dve.wait_ge(gram_done, b + 1)
                nc.vector.tensor_tensor(band[:, :, :], const[:, C_BAND:C_BAND + 3 * BAND]
                                        .rearrange("p (l k) -> p l k", l=3),
                                        gb[:, 0:BAND].unsqueeze(1).to_broadcast([P, 3, BAND]),
                                        ALU.mult).then_inc(gram_step, 1)
                dve.wait_ge(gram_step, GRAM_STEPS * b + 1)
                nc.vector.reduce_sum(gram[:, :], band[:, :, :], AX.X).then_inc(gram_side, 1)

            def gram_softmax_in(b):
                def then(ins, n):
                    ins.then_inc(gram_step, 1)
                    dve.wait_ge(gram_step, GRAM_STEPS * b + n)
                dve.wait_ge(gram_side, b + 1)
                flat = gram_e[:, :, :].rearrange("p s l -> p (s l)")
                nc.vector.tensor_tensor(flat[:, 0:3], gram[:, :], const[:, C_END:C_END + 3], ALU.add)
                dve.wait_ge(shift_done, b + 1)
                then(nc.vector.tensor_tensor(flat[:, 3:4], gb[:, SHIFT:SHIFT + 1], const[:, C_END + 3:C_END + 4],
                                             ALU.add), 2)
                then(nc.vector.reduce_max(pair_max[:, :], gram_e[:, :, :], AX.X), 3)
                nc.vector.tensor_tensor(gram_d[:, :, :], gram_e[:, :, :],
                                        pair_max[:, :].unsqueeze(2).to_broadcast([P, 2, 2]),
                                        ALU.subtract).then_inc(gram_ready, 1)

            def gram_softmax_out(b):
                def then(ins, n):
                    ins.then_inc(gram_step, 1)
                    dve.wait_ge(gram_step, GRAM_STEPS * b + n)
                dve.wait_ge(gram_exp, b + 1)
                then(nc.vector.reduce_sum(pair_sum[:, :], gram_x[:, :, :], AX.X), 4)
                then(nc.vector.reciprocal(pair_inv[:, :], pair_sum[:, :]), 5)
                then(nc.vector.tensor_tensor(catt[:, :, :], gram_x[:, :, :],
                                             pair_inv[:, :].unsqueeze(2).to_broadcast([P, 2, 2]), ALU.mult), 6)
                before = (const[:, C_DOWN:C_DOWN + P], ident)
                after = (ident, const[:, C_UP:C_UP + P])
                for s in range(2):
                    last = nc.vector.tensor_scalar(mixer_part[:, s, :], before[s], catt[:, s, 0:1], None, ALU.mult)
                then(last, 7)
                for s in range(2):
                    last = nc.vector.scalar_tensor_tensor(mixer[:, s, :], after[s], catt[:, s, 1:2],
                                                          mixer_part[:, s, :], ALU.mult, ALU.add)
                last.then_inc(mixer_done, 1)

            GRAM_STEPS = 7

            def attend(b):
                gram_pick(b)
                maxima(b, 0)
                maxima(b, 1)
                gram_softmax_in(b)
                maxima(b, 2)
                gram_softmax_out(b)
                maxima(b, 3)

            def finish(b):
                dve.wait_ge(exp_done, QUARTERS * (b + 1))
                nc.vector.reciprocal(row_inv[:, :, :], row_sum[:, :, :]).then_inc(inv_done, 1)
                dve.wait_ge(inv_done, b + 1)
                weigh(b, 0)
                for q in range(QUARTERS):
                    for h in range(HALF):
                        dve.wait_ge(ez_done, 2 * (QUARTERS * b + q) + h + 1)
                        nc.vector.tensor_scalar(elu[h][:, :], elu[h][:, :], 1.0, None, ALU.min).then_inc(clip_done, 1)
                        dve.wait_ge(clip_done, 2 * (QUARTERS * b + q) + h + 1)
                        nc.vector.scalar_tensor_tensor(elu[h][:, :], z[h][:, :], 1.0, elu[h][:, :],
                                                       ALU.add, ALU.max).then_inc(elu_done[h], 1)
                    if q + 1 < QUARTERS:
                        weigh(b, q + 1)
                    for h in range(HALF):
                        dve.wait_ge(keep_done, QUARTERS * b + q + 1)
                        dve.wait_ge(elu_done[h], QUARTERS * b + q + 1)
                        nc.vector.scalar_tensor_tensor(blend[q % 2][:, h, :], elu[h][:, :], vec[:, 8:9],
                                                       blend[q % 2][:, h, :], ALU.mult, ALU.add)\
                            .then_inc(blend_done[h], 1)

            dve.wait_ge(const_in, 48)
            nc.vector.tensor_copy(ident_b[:, :], ident).then_inc(casts_done, 1)
            nc.vector.tensor_copy(mask_b[:, :], const[:, C_MASK:C_MASK + MASKS]).then_inc(casts_done, 1)
            part = vec[:, 0:8].rearrange("p (s n) -> p n s", s=2)
            chain(nc.vector.tensor_scalar(bn[:, 0, :], part[:, 3, :], 1e-5, None, ALU.add))
            nc.vector.tensor_scalar(mix[:, 0:1], vec[:, 8:9], -1.0, 1.0, ALU.mult, ALU.add)
            nc.vector.tensor_scalar(mix[:, 1:2], vec[:, 8:9], -1.0, None, ALU.mult).then_inc(bn_var, 1)
            dve.wait_ge(bn_root, 1)
            chain(nc.vector.reciprocal(bn[:, 2, :], bn[:, 1, :]))
            chain(nc.vector.tensor_tensor(bn[:, 3, :], bn[:, 0, :], bn[:, 2, :], ALU.mult))
            chain(nc.vector.tensor_tensor(bn[:, 4, :], bn[:, 1, :], bn[:, 3, :], ALU.add))
            chain(nc.vector.tensor_scalar(bn[:, 3, :], bn[:, 4, :], 0.5, None, ALU.mult))
            chain(nc.vector.reciprocal(bn[:, 5, :], bn[:, 3, :]))
            chain(nc.vector.tensor_tensor(bn[:, 6, :], part[:, 0, :], bn[:, 5, :], ALU.mult))
            chain(nc.vector.tensor_tensor(bn[:, 2, :], part[:, 2, :], bn[:, 6, :], ALU.mult))
            nc.vector.tensor_tensor(bn[:, 7, :], part[:, 1, :], bn[:, 2, :], ALU.subtract).then_inc(bn_done, 1)
            for h in range(HALF):
                dve.sem_inc(blend_done[h], FREE)
            attend(0)
            with dve.Fori(0, B // BUFS) as k:
                for j in range(BUFS):
                    b = k * BUFS + j
                    finish(b)
                    attend(b + 1)
            finish(B - 1)

        @block.tensor
        def _(pe):
            def mm(o, l, r, start, stop, **kw):
                return nc.tensor.matmul(o, l, r, start=start, stop=stop, skip_group_check=True, **kw)

            def transpose_x(b, j, q, first):
                xb = xs[j]
                if q == QUARTERS - 1 and not first:
                    pe.wait_ge(pt_out, QUARTERS * b)
                for t in range(2):
                    g = 2 * q + t
                    if q > 0:
                        pe.wait_ge(xt_out, EVACS * b + g - 1)
                    elif not first:
                        pe.wait_ge(proj_out, 3 * b - 1 + t)
                    for v in range(2):
                        for h in range(HALF):
                            at0 = (2 * g + v) * WIN
                            last = nc.tensor.transpose(xp[t][:, v * C + h * P:v * C + (h + 1) * P],
                                                       xb[:, h, at0:at0 + WIN], ident)
                    last.then_inc(xt_done, 1)
                    if g == EVACS - 3:
                        for h in range(HALF):
                            last = nc.tensor.transpose(et[0:64, h * P:(h + 1) * P],
                                                       xb[:, h, GROUPS * WIN:GROUPS * WIN + 64], ident)
                        last.then_inc(xt_done, 1)

            def gram_band(b, q, first):
                last_q = q == QUARTERS - 1
                pe.wait_ge(xt_out, EVACS * b + (EVACS if last_q else 2 * (q + 1)))
                if q == 0 and not first:
                    pe.wait_ge(mt_out, b)
                for v in range(q * GQ, (q + 1) * GQ + last_q):
                    k = P if v < GROUPS else P // 2
                    for blk in range(P // HID):
                        mine, other = blk * HID, P + blk * HID - 1
                        last = mm(gb[mine:mine + HID, 0:BAND], upper[0:k, v, mine:mine + HID],
                                  upper[0:k, v, other:other + BAND], v == 0, v == GROUPS, tile_position=(0, mine))
                if last_q:
                    last.then_inc(gram_done, 1)

            def shift_gram(b):
                pe.wait_ge(gram_side, b + 1)
                mm(gb[:, SHIFT:SHIFT + 1], const[:, C_DOWN:C_DOWN + P], gram[:, 0:1], True, True)\
                    .then_inc(shift_done, 1)

            def project(b, j, first):
                xb = xs[j]
                if not first:
                    pe.wait_ge(hs_out, SUMS * b - 1)
                for h in range(HALF):
                    for q in range(QUARTERS):
                        last = mm(pj[q * HID:(q + 1) * HID, :], wt[:, h, 0:HID], xb[:, h, W + q * QN:W + (q + 1) * QN],
                                  h == 0, h == HALF - 1, tile_position=(0, q * HID))
                last.then_inc(proj_done, 1)
                pe.wait_ge(xt_out, EVACS * b + EVACS)
                for h in range(HALF):
                    for q in range(QUARTERS):
                        last = mm(xp[0][q * HID:(q + 1) * HID, :], wt[:, h, HID:], xb[:, h, W + q * QN:W + (q + 1) * QN],
                                  h == 0, h == HALF - 1, tile_position=(0, q * HID))
                last.then_inc(proj_done, 1)
                for h in range(HALF):
                    rows = xb[:, h, :].rearrange("p (r w) -> p r w", w=W)
                    for q in range(QUARTERS):
                        last = mm(xp[1][q * HID:(q + 1) * HID, 0:2 * W], wt[:, h, HID:],
                                  rows[:, q * QR:q * QR + QR + 2:QR + 1, :],
                                  h == 0, h == HALF - 1, tile_position=(0, q * HID))
                last.then_inc(proj_done, 1)

            def scores(b, q, first):
                if q == 0:
                    pe.wait_ge(proj_out, 3 * b + 3)
                    if not first:
                        pe.wait_ge(hs_out, SUMS * b)
                elif q < 3:
                    if not first:
                        pe.wait_ge(elu_done[q - 1], QUARTERS * b)
                else:
                    pe.wait_ge(exp_done, QUARTERS * b + 1)
                m0 = (q > 0) * WIN + (q == QUARTERS - 1) * WIN
                mm(score[q][:, :], ident_b[:, :], mask_b[:, m0:m0 + GQ * WIN], True, False)
                lo = q * HID
                for v in range(GQ):
                    for c in range(2):
                        last = mm(score[q][c * 64:(c + 1) * 64, v * WIN:(v + 1) * WIN],
                                  query[lo:lo + HID, v * WIN + c * NQ:v * WIN + (c + 1) * NQ],
                                  key[lo:lo + HID, v * WIN + c * 2 * W:v * WIN + c * 2 * W + WIN],
                                  False, True, tile_position=(lo, c * 64))
                last.then_inc(score_done, 1)

            def transpose_probs(b, q):
                pe.wait_ge(exp_done, QUARTERS * b + q + 1)
                if q > 0:
                    pe.wait_ge(pt_out, QUARTERS * b + q)
                else:
                    pe.wait_ge(xt_out, EVACS * (b + 1))
                for v in range(GQ):
                    last = nc.tensor.transpose(et[:, v * P:(v + 1) * P], probs[q % 2][:, v, :], ident)
                last.then_inc(pt_done, 1)

            def transpose_mixer(b):
                pe.wait_ge(mixer_done, b + 1)
                for s in range(2):
                    last = nc.tensor.transpose(gb[:, (1 + s) * P:(2 + s) * P], mixer[:, s, :], ident)
                last.then_inc(mt_done, 1)

            def attend(b, j, first=False):
                project(b, j, first)
                gram_band(b, 3, first)
                scores(b, 0, first)
                scores(b, 1, first)
                shift_gram(b)
                scores(b, 2, first)
                transpose_probs(b, 0)
                scores(b, 3, first)
                transpose_mixer(b)
                transpose_probs(b, 1)

            def channel_sums(b, j, q, h):
                if q == 0:
                    pe.wait_ge(mt_out, b + 1)
                    pe.wait_ge(exp_done, QUARTERS * b + h + 2)
                else:
                    pe.wait_ge(elu_done[h], QUARTERS * b + q)
                mm(z[h][:, :], mixer_t[:, h * P:(h + 1) * P], xs[j][:, 1 - h, W + q * QN:W + (q + 1) * QN],
                   True, False)

            def window_sums(b, q, t):
                pe.wait_ge(pt_out, QUARTERS * b + q + 1)
                if t == 0:
                    pe.wait_ge(lower_in[q], 32 * (b + 1))
                    if q + 1 < QUARTERS:
                        pe.wait_ge(lower_in[q + 1], 32 * (b + 1))
                if q > 0:
                    pe.wait_ge(hs_out, SUMS * b + PARTS * (q - 1) + t + 1)
                elif t == 1:
                    pe.wait_ge(exp_done, QUARTERS * (b + 1))
                for i in range(GV):
                    v = t * GV + i
                    for c, window in enumerate((upper, lower)):
                        last = mm(part_bank[t][c * NQ:(c + 1) * NQ, i * C:(i + 1) * C],
                                  probs_t[:, q, v * P + c * NQ:v * P + (c + 1) * NQ],
                                  window[:, q * GQ + v, :], True, True, tile_position=(0, c * NQ))
                last.then_inc(hs_done, 1)

            def add_spatial(b, q, h):
                for t in range(PARTS):
                    pe.wait_ge(hs_out, SUMS * b + PARTS * q + t + 1)
                    for v in range(t * GV, (t + 1) * GV):
                        last = mm(z[h][:, v * P:(v + 1) * P], spatial[:, v, h * P:(h + 1) * P], ident,
                                  False, v == GQ - 1, is_transpose=True)
                last.then_inc(z_done, 1)

            def finish(b, j, n=None, n_loaded=None):
                channel_sums(b, j, 0, 0)
                transpose_probs(b, 2)
                channel_sums(b, j, 0, 1)
                window_sums(b, 0, 0)
                transpose_probs(b, 3)
                window_sums(b, 0, 1)
                add_spatial(b, 0, 0)
                add_spatial(b, 0, 1)
                if n is not None:
                    pe.wait_ge(x_in[n], n_loaded)
                for q in range(QUARTERS):
                    if n is not None:
                        transpose_x(b + 1, n, q, False)
                    if q + 1 < QUARTERS:
                        window_sums(b, q + 1, 0)
                        window_sums(b, q + 1, 1)
                        channel_sums(b, j, q + 1, 0)
                        channel_sums(b, j, q + 1, 1)
                        if n is not None:
                            gram_band(b + 1, q, False)
                        add_spatial(b, q + 1, 0)
                        add_spatial(b, q + 1, 1)

            pe.wait_ge(const_in, 48)
            pe.wait_ge(casts_done, 2)
            pe.wait_ge(x_in[0], 16)
            for q in range(QUARTERS):
                transpose_x(0, 0, q, True)
                if q < QUARTERS - 1:
                    gram_band(0, q, True)
            attend(0, 0, True)
            with pe.Fori(0, B // BUFS) as k:
                for j in range(BUFS):
                    b = k * BUFS + j
                    n = (j + 1) % BUFS
                    finish(b, j, n, 16 * (k + 1 + (j + 1) // BUFS))
                    attend(b + 1, n)
            finish(B - 1, (B - 1) % BUFS)


def shape_constants():
    import numpy as np
    const = np.zeros((P, C_ALL), np.float32)
    i = np.arange(P)
    const[i, C_ID + i] = 1.0
    const[i[1:], C_DOWN + i[:-1]] = 1.0
    const[i[:-1], C_UP + i[1:]] = 1.0
    const[i, C_BAND + i % HID] = 1.0
    const[0, C_BAND] = 0.0
    for n in range(1, 3):
        const[i, C_BAND + n * BAND + i % HID + 1] = 1.0
    const[0, C_END] = NEG
    const[P - 1, C_END + 3] = NEG
    kind, query_row, query_col = i // NQ, (i // W) % 2 + 1, i % W
    key_row, key_col = np.arange(WIN) // W, np.arange(WIN) % W
    di = abs(query_row[:, None] - key_row)
    dj = abs(query_col[:, None] - key_col)
    near = (di <= 1) & (dj <= 1) & ~((di == 0) & (dj == 0))
    for n in range(6):
        inside = np.ones((P, WIN), bool)
        if n == 0:
            inside &= ~((kind[:, None] == 0) & (key_row == 0))
        if n == 5:
            inside &= ~((kind[:, None] == 1) & (key_row == WR - 1))
        const[:, C_MASK + n * WIN:C_MASK + (n + 1) * WIN] = np.where(near & inside, 0.0, NEG)
    return const


def kernel(**inputs):
    import numpy as np
    import concourse.bacc as bacc
    from concourse.bass_utils import run_bass_kernel_spmd

    a = {name.replace("L0_conv_", ""): np.asarray(v) for name, v in inputs.items()}
    w_t = np.concatenate([a["wa"], a["ws"]], axis=0).T.reshape(P, HALF, 2 * HID)
    norms = np.stack([a[n + s] for s in "as" for n in "gbmv"], axis=1)
    vectors = np.concatenate([np.tile(norms, (QUARTERS, 1)), np.tile(a["gama"].reshape(1, 1), (P, 1))], axis=1)
    arrays = {"x_dram": a["x"], "w_dram": w_t, "vectors_dram": vectors, "constants_dram": shape_constants()}
    arrays = {name: np.ascontiguousarray(v) for name, v in arrays.items()}

    nc = bacc.Bacc("TRN2", target_bir_lowering=False, num_devices=1)
    args = [nc.dram_tensor(name, v.shape, mybir.dt.from_np(v.dtype), kind="ExternalInput").ap()
            for name, v in arrays.items()]
    out = nc.dram_tensor("out_dram", (B, C, H, W), mybir.dt.float32, kind="ExternalOutput").ap()
    graph_attention(nc, *args, out)
    result = run_bass_kernel_spmd(nc, [arrays], core_ids=[0])
    return result.results[0]["out_dram"]
```

```python
from contextlib import ExitStack

import concourse.bass as bass
from concourse import mybir

B, C, H, W = 16, 256, 64, 32
HID = C // 8
P = 128
HALF = C // P
N = H * W
QUARTERS = P // HID
QR = H // QUARTERS
QN = QR * W
WR = 4
WIN = WR * W
NQ = WIN // 2
GROUPS = N // WIN
GQ = GROUPS // QUARTERS
BUFS = 3
FREE = 2
NEG = -9000000000000000.0
BAND = HID + 1
EVACS = GROUPS // 2 + 1
PARTS = 2
GV = GQ // PARTS
SUMS = PARTS * QUARTERS
SHIFT = 400

C_ID, C_DOWN = 0, P
C_BAND = 2 * P
C_END = C_BAND + 3 * BAND
C_MASK = C_END + 4
MASKS = 6 * WIN
C_ALL = C_MASK + MASKS


def graph_attention(nc, x, w_t, vectors, constants, out):
    fp32, bf16 = mybir.dt.float32, mybir.dt.bfloat16
    ALU = mybir.AluOpType
    ACT = mybir.ActivationFunctionType
    AX = mybir.AxisListType

    x_img = x.rearrange("b (p h) r w -> b p h (r w)", h=HALF)
    out_img = out.rearrange("b (p h) r w -> b p h (r w)", h=HALF)

    ctx = ExitStack()
    with ctx:
        def sb(name, shape, dt=fp32):
            return ctx.enter_context(nc.sbuf_tensor(name, shape, dt))

        def bank(name):
            return ctx.enter_context(nc.psum_tensor(name, [P, 512], fp32))

        def sem(name):
            return ctx.enter_context(nc.semaphore(name))

        xs = [sb(f"x{j}", [P, HALF, N + 2 * W]) for j in range(BUFS)]
        near = [sb(f"near{j}", [P, HALF, N]) for j in range(BUFS)]
        upper = sb("upper", [P, GROUPS + 1, C])
        lower = sb("lower", [P, GROUPS, C])
        const = sb("const", [P, C_ALL])
        ident_b = sb("ident_b", [P, P], bf16)
        mask_b = sb("mask_b", [P, MASKS], bf16)
        wt = sb("wt", [P, HALF, 2 * HID])
        vec = sb("vec", [P, 9])
        bn = sb("bn", [P, 8, 2])
        mix = sb("mix", [P, 2])
        query = sb("query", [P, QN])
        key = sb("key", [P, QN + 2 * W])
        neg_max = sb("neg_max", [P, QUARTERS, GQ])
        row_sum = sb("row_sum", [P, QUARTERS, GQ])
        row_inv = sb("row_inv", [P, QUARTERS, GQ])
        probs = [sb(f"probs{i}", [P, GQ, WIN]) for i in range(2)]
        probs_t = sb("probs_t", [P, QUARTERS, GQ * P])
        spatial = [sb(f"spatial{i}", [P, GQ, C]) for i in range(2)]
        band = sb("band", [P, 3, BAND])
        gram = sb("gram", [P, 3])
        gram_e = sb("gram_e", [P, 2, 2])
        pair_max = sb("pair_max", [P, 2])
        gram_d = sb("gram_d", [P, 2, 2])
        gram_x = sb("gram_x", [P, 2, 2])
        pair_sum = sb("pair_sum", [P, 2])
        pair_inv = sb("pair_inv", [P, 2])
        catt = sb("catt", [P, 2, 2])
        product = [sb(f"product{h}", [P, QN]) for h in range(HALF)]
        elu = [sb(f"elu{i}", [P, HALF, QN]) for i in range(2)]
        blend = [sb(f"blend{q}", [P, HALF, QN]) for q in range(QUARTERS)]

        xp = [bank("xp0"), bank("xp1")]
        pj = bank("pj")
        gb = bank("gb")
        et = bank("et")
        at = bank("at")
        z = [bank("z0"), bank("z1")]
        score = [xp[0], at, z[0], z[1]]
        part_bank = [pj, at]

        const_in = sem("const_in")
        x_in = [sem(f"x_in{j}") for j in range(BUFS)]
        first_in = [sem(f"first_in{q}") for q in range(QUARTERS)]
        pads_done = sem("pads_done")
        casts_done = sem("casts_done")
        bn_step = sem("bn_step")
        bn_var = sem("bn_var")
        bn_root = sem("bn_root")
        bn_done = sem("bn_done")
        xt_done = sem("xt_done")
        xt_out = sem("xt_out")
        lower_in = [sem(f"lower_in{q}") for q in range(QUARTERS)]
        gram_done = sem("gram_done")
        proj_done = sem("proj_done")
        proj_out = sem("proj_out")
        score_done = sem("score_done")
        max_done = sem("max_done")
        exp_done = sem("exp_done")
        inv_done = sem("inv_done")
        pt_done = sem("pt_done")
        pt_out = sem("pt_out")
        hs_done = sem("hs_done")
        hs_out = sem("hs_out")
        gram_step = sem("gram_step")
        gram_side = sem("gram_side")
        shift_done = sem("shift_done")
        gram_ready = sem("gram_ready")
        gram_exp = sem("gram_exp")
        catt_done = sem("catt_done")
        near_in = [sem(f"near_in{j}") for j in range(BUFS)]
        near_zero = sem("near_zero")
        product_done = sem("product_done")
        channel_done = sem("channel_done")
        z_done = sem("z_done")
        ez_done = sem("ez_done")
        clip_done = sem("clip_done")
        elu_done = [sem(f"elu_done{h}") for h in range(HALF)]
        keep_done = sem("keep_done")
        gama_done = sem("gama_done")
        blend_done = sem("blend_done")
        stored = [sem(f"stored{q}") for q in range(QUARTERS)]

        block = ctx.enter_context(nc.Block())
        ident = const[:, C_ID:C_ID + P]

        @block.sync
        def _(sp):
            def load_x(b, j):
                sp.dma_start(xs[j][:, :, W:W + N], x_img[b]).then_inc(x_in[j], 16)

            def build_near(j, loaded):
                sp.wait_ge(x_in[j], loaded)
                sp.dma_start(near[j][1:P, 0, :], xs[j][0:P - 1, 1, W:W + N]).then_inc(near_in[j], 16)
                sp.dma_start(near[j][0:P - 1, 1, :], xs[j][1:P, 0, W:W + N]).then_inc(near_in[j], 16)

            def build_lower(b, q):
                v0 = q * GQ
                sp.wait_ge(xt_out, EVACS * b + (EVACS if q == QUARTERS - 1 else 2 * (q + 1)))
                sp.dma_start(lower[0:64, v0:v0 + GQ, :], upper[64:128, v0:v0 + GQ, :]).then_inc(lower_in[q], 16)
                first, last = max(v0, 1), v0 + GQ + (q == QUARTERS - 1)
                sp.dma_start(lower[64:128, first - 1:last - 1, :], upper[0:64, first:last, :])\
                    .then_inc(lower_in[q], 16)

            def store(b, q):
                sp.wait_ge(blend_done, FREE + QUARTERS * b + q + 1)
                sp.dma_start(out_img[b, :, :, q * QN:(q + 1) * QN], blend[q][:, :, :])\
                    .then_inc(stored[q], 16)

            def image(b, j, load, loaded=None):
                for q in range(QUARTERS):
                    build_lower(b + 1, q)
                    store(b, q)
                    if q == 0 and loaded is not None:
                        build_near((j + 2) % BUFS, loaded)
                if load:
                    load_x(b + BUFS, j)

            sp.dma_start(const[:, :], constants).then_inc(const_in, 16)
            sp.dma_start(vec[:, :], vectors).then_inc(const_in, 16)
            sp.dma_start(wt[:, :, :], w_t).then_inc(const_in, 16)
            sp.wait_ge(pads_done, BUFS * 2)
            for q in range(QUARTERS):
                sp.dma_start(xs[0][:, :, W + q * QN:W + (q + 1) * QN], x_img[0][:, :, q * QN:(q + 1) * QN])\
                    .then_inc(first_in[q], 16)
            load_x(1, 1)
            load_x(2, 2)
            for q in range(QUARTERS):
                sp.wait_ge(first_in[q], 16)
            sp.sem_inc(x_in[0], 16)
            sp.wait_ge(near_zero, BUFS)
            build_near(0, 16)
            for q in range(QUARTERS):
                build_lower(0, q)
            build_near(1, 16)
            with sp.Fori(0, B // BUFS - 1) as k:
                for j in range(BUFS):
                    image(k * BUFS + j, j, True, 16 * (k + 1 + (j + 2) // BUFS))
            for b in range(B - B % BUFS - BUFS, B - 1):
                image(b, b % BUFS, b + BUFS < B, 16 * ((b + 2) // BUFS + 1) if b + 2 < B else None)
            for q in range(QUARTERS):
                store(B - 1, q)
            for q in range(QUARTERS):
                sp.wait_ge(stored[q], 16 * (FREE + B))

        @block.gpsimd
        def _(pool):
            for j in range(BUFS):
                nc.gpsimd.memset(xs[j][:, :, 0:W], 0.0).then_inc(pads_done, 1)
                nc.gpsimd.memset(xs[j][:, :, W + N:], 0.0).then_inc(pads_done, 1)
            for j in range(BUFS):
                nc.gpsimd.memset(near[j][:, :, :], 0.0).then_inc(near_zero, 1)
            for q in range(QUARTERS):
                pool.sem_inc(stored[q], 16 * FREE)
            pool.sem_inc(blend_done, FREE)

            def blend_x(b):
                for q in range(QUARTERS):
                    pool.wait_ge(keep_done, QUARTERS * b + q + 1)
                    pool.wait_ge(gama_done, QUARTERS * b + q + 1)
                    nc.gpsimd.tensor_tensor(blend[q][:, :, :], elu[q % 2][:, :, :], blend[q][:, :, :],
                                            ALU.add).then_inc(blend_done, 1)

            with pool.Fori(0, B // BUFS) as k:
                for j in range(BUFS):
                    blend_x(k * BUFS + j)
            blend_x(B - 1)

        @block.scalar
        def _(act):
            def move_xt(b, q):
                for t in range(2):
                    g = 2 * q + t
                    act.wait_ge(xt_done, EVACS * b + g + 1 + (g == EVACS - 2))
                    nc.scalar.activation(upper[:, 2 * g:2 * g + 2, :], xp[t][:, :].rearrange("p (v c) -> p v c", v=2),
                                         ACT.Copy).then_inc(xt_out, 1)
                    if g == EVACS - 3:
                        act.wait_ge(xt_done, EVACS * b + g + 2)
                        nc.scalar.activation(upper[0:64, GROUPS, :], et[0:64, 0:C], ACT.Copy).then_inc(xt_out, 1)

            def exp_z(b, q):
                for h in range(HALF):
                    act.wait_ge(z_done, 2 * (QUARTERS * b + q) + h + 1)
                    act.wait_ge(blend_done, FREE + QUARTERS * b + q - 1)
                    nc.scalar.activation(elu[q % 2][:, h, :], z[h][:, :], ACT.Exp).then_inc(ez_done, 1)

            def times_gama(b, q):
                for h in range(HALF):
                    act.wait_ge(elu_done[h], QUARTERS * b + q + 1)
                nc.scalar.activation(elu[q % 2][:, :, :], elu[q % 2][:, :, :], ACT.Identity,
                                     scale=vec[:, 8:9]).then_inc(gama_done, 1)

            def weigh_own(b, j, q):
                for h in range(HALF):
                    if q == 0:
                        act.wait_ge(catt_done, b + 1)
                    nc.scalar.activation(product[h][:, :], xs[j][:, 1 - h, W + q * QN:W + (q + 1) * QN], ACT.Identity,
                                         scale=catt[:, h, 1 - h:2 - h]).then_inc(product_done, 1)

            def keep_x(b, j, q):
                act.wait_ge(stored[q], 16 * (FREE + b))
                nc.scalar.activation(blend[q][:, :, :], xs[j][:, :, W + q * QN:W + (q + 1) * QN], ACT.Identity,
                                     bias=mix[:, 1:2], scale=mix[:, 0:1]).then_inc(keep_done, 1)

            def exp_scores(b, q):
                act.wait_ge(max_done, QUARTERS * b + q + 1)
                if not (isinstance(b, int) and b == 0 and q < 2):
                    act.wait_ge(pt_done, QUARTERS * b + q - 1)
                for v in range(GQ):
                    last = nc.scalar.activation(probs[q % 2][:, v, :], score[q][:, v * WIN:(v + 1) * WIN], ACT.Exp,
                                                bias=neg_max[:, q, v:v + 1], accum_out=row_sum[:, q, v:v + 1])
                last.then_inc(exp_done, 1)

            def query_out(b):
                act.wait_ge(proj_done, 3 * b + 1)
                nc.scalar.activation(query[:, :], pj[:, :], ACT.Relu, bias=bn[:, 7, 0:1], scale=bn[:, 6, 0:1])\
                    .then_inc(proj_out, 1)

            def attend(b, j, first=False):
                act.wait_ge(proj_done, 3 * b + 2)
                nc.scalar.activation(key[:, W:W + QN], at[:, :], ACT.Relu, bias=bn[:, 7, 1:2],
                                     scale=bn[:, 6, 1:2]).then_inc(proj_out, 1)
                act.wait_ge(proj_done, 3 * b + 3)
                nc.scalar.activation(key[:, :].rearrange("p (r w) -> p r w", w=W)[:, 0:QR + 2:QR + 1, :],
                                     pj[:, 0:2 * W].rearrange("p (r w) -> p r w", w=W), ACT.Relu,
                                     bias=bn[:, 7, 1:2], scale=bn[:, 6, 1:2]).then_inc(proj_out, 1)
                keep_x(b, j, 0)
                if not first:
                    exp_z(b - 1, QUARTERS - 1)
                exp_scores(b, 0)
                if not first:
                    times_gama(b - 1, QUARTERS - 1)
                exp_scores(b, 1)
                act.wait_ge(gram_ready, b + 1)
                nc.scalar.activation(gram_x[:, :, :], gram_d[:, :, :], ACT.Exp).then_inc(gram_exp, 1)
                exp_scores(b, 2)
                exp_scores(b, 3)

            act.wait_ge(bn_var, 1)
            nc.scalar.activation(bn[:, 1, :], bn[:, 0, :], ACT.Sqrt).then_inc(bn_root, 1)
            act.wait_ge(bn_done, 1)
            for q in range(QUARTERS):
                move_xt(0, q)
            act.wait_ge(x_in[0], 16)
            query_out(0)
            attend(0, 0, True)
            with act.Fori(0, B // BUFS) as k:
                for j in range(BUFS):
                    b = k * BUFS + j
                    weigh_own(b, j, 0)
                    keep_x(b, j, 1)
                    keep_x(b, j, 2)
                    for q in range(QUARTERS - 2):
                        exp_z(b, q)
                        weigh_own(b, j, q + 1)
                        move_xt(b + 1, q)
                        times_gama(b, q)
                    exp_z(b, 2)
                    move_xt(b + 1, 2)
                    weigh_own(b, j, 3)
                    keep_x(b, j, 3)
                    query_out(b + 1)
                    move_xt(b + 1, 3)
                    times_gama(b, 2)
                    n = (j + 1) % BUFS
                    act.wait_ge(x_in[n], 16 * (k + 1 + (j + 1) // BUFS))
                    attend(b + 1, n)
            last = (B - 1) % BUFS
            weigh_own(B - 1, last, 0)
            keep_x(B - 1, last, 1)
            keep_x(B - 1, last, 2)
            keep_x(B - 1, last, 3)
            for q in range(QUARTERS):
                exp_z(B - 1, q)
                if q + 1 < QUARTERS:
                    weigh_own(B - 1, last, q + 1)
                times_gama(B - 1, q)

        @block.vector
        def _(dve):
            steps = [0]

            def chain(ins):
                steps[0] += 1
                ins.then_inc(bn_step, 1)
                dve.wait_ge(bn_step, steps[0])

            def maxima(b, q):
                dve.wait_ge(score_done, QUARTERS * b + q + 1)
                nc.vector.reduce_max(neg_max[:, q, :], score[q][:, :].rearrange("p (v m) -> p v m", m=WIN), AX.X,
                                     negate=True).then_inc(max_done, 1)

            def move_probs(b, q):
                dve.wait_ge(pt_done, QUARTERS * b + q + 1)
                nc.vector.tensor_copy(probs_t[:, q, :], et[:, :]).then_inc(pt_out, 1)

            def invert_sums(b, i):
                dve.wait_ge(exp_done, QUARTERS * b + 2 * (i + 1))
                nc.vector.reciprocal(row_inv[:, 2 * i:2 * i + 2, :], row_sum[:, 2 * i:2 * i + 2, :])\
                    .then_inc(inv_done, 1)

            def weigh(b, q, t):
                dve.wait_ge(inv_done, 2 * b + q // 2 + 1)
                dve.wait_ge(hs_done, SUMS * b + PARTS * q + t + 1)
                nc.vector.tensor_tensor(spatial[q % 2][:, t * GV:(t + 1) * GV, :],
                                        part_bank[t][:, :].rearrange("p (v c) -> p v c", v=GV),
                                        row_inv[:, q, t * GV:(t + 1) * GV].unsqueeze(2).to_broadcast([P, GV, C]),
                                        ALU.mult).then_inc(hs_out, 1)

            def mix_channels(b, j, q, h):
                dve.wait_ge(product_done, 2 * (QUARTERS * b + q) + h + 1)
                nc.vector.scalar_tensor_tensor(z[h][:, :], near[j][:, h, q * QN:(q + 1) * QN], catt[:, h, h:h + 1],
                                               product[h][:, :], ALU.mult, ALU.add).then_inc(channel_done, 1)

            def elu_out(b, q):
                for h in range(HALF):
                    dve.wait_ge(ez_done, 2 * (QUARTERS * b + q) + h + 1)
                    nc.vector.tensor_scalar(elu[q % 2][:, h, :], elu[q % 2][:, h, :], 1.0, None, ALU.min)\
                        .then_inc(clip_done, 1)
                for h in range(HALF):
                    dve.wait_ge(clip_done, 2 * (QUARTERS * b + q) + h + 1)
                    nc.vector.scalar_tensor_tensor(elu[q % 2][:, h, :], z[h][:, :], 1.0, elu[q % 2][:, h, :],
                                                   ALU.add, ALU.max).then_inc(elu_done[h], 1)

            def gram_pick(b):
                dve.wait_ge(gram_done, b + 1)
                nc.vector.tensor_tensor(band[:, :, :], const[:, C_BAND:C_BAND + 3 * BAND]
                                        .rearrange("p (l k) -> p l k", l=3),
                                        gb[:, 0:BAND].unsqueeze(1).to_broadcast([P, 3, BAND]),
                                        ALU.mult).then_inc(gram_step, 1)
                dve.wait_ge(gram_step, GRAM_STEPS * b + 1)
                nc.vector.reduce_sum(gram[:, :], band[:, :, :], AX.X).then_inc(gram_side, 1)

            def gram_softmax_in(b):
                def then(ins, n):
                    ins.then_inc(gram_step, 1)
                    dve.wait_ge(gram_step, GRAM_STEPS * b + n)
                dve.wait_ge(gram_side, b + 1)
                flat = gram_e[:, :, :].rearrange("p s l -> p (s l)")
                nc.vector.tensor_tensor(flat[:, 0:3], gram[:, :], const[:, C_END:C_END + 3], ALU.add)
                dve.wait_ge(shift_done, b + 1)
                then(nc.vector.tensor_tensor(flat[:, 3:4], gb[:, SHIFT:SHIFT + 1], const[:, C_END + 3:C_END + 4],
                                             ALU.add), 2)
                then(nc.vector.reduce_max(pair_max[:, :], gram_e[:, :, :], AX.X), 3)
                nc.vector.tensor_tensor(gram_d[:, :, :], gram_e[:, :, :],
                                        pair_max[:, :].unsqueeze(2).to_broadcast([P, 2, 2]),
                                        ALU.subtract).then_inc(gram_ready, 1)

            def gram_softmax_out(b):
                def then(ins, n):
                    ins.then_inc(gram_step, 1)
                    dve.wait_ge(gram_step, GRAM_STEPS * b + n)
                dve.wait_ge(gram_exp, b + 1)
                then(nc.vector.reduce_sum(pair_sum[:, :], gram_x[:, :, :], AX.X), 4)
                then(nc.vector.reciprocal(pair_inv[:, :], pair_sum[:, :]), 5)
                nc.vector.tensor_tensor(catt[:, :, :], gram_x[:, :, :],
                                        pair_inv[:, :].unsqueeze(2).to_broadcast([P, 2, 2]),
                                        ALU.mult).then_inc(catt_done, 1)

            GRAM_STEPS = 5

            def attend(b, first=False):
                gram_pick(b)
                maxima(b, 0)
                if not first:
                    elu_out(b - 1, QUARTERS - 1)
                maxima(b, 1)
                gram_softmax_in(b)
                move_probs(b, 0)
                maxima(b, 2)
                gram_softmax_out(b)
                maxima(b, 3)
                move_probs(b, 1)

            def finish(b, j, loaded):
                dve.wait_ge(near_in[j], loaded)
                invert_sums(b, 0)
                weigh(b, 0, 0)
                weigh(b, 0, 1)
                move_probs(b, 2)
                weigh(b, 1, 0)
                mix_channels(b, j, 0, 0)
                move_probs(b, 3)
                mix_channels(b, j, 0, 1)
                weigh(b, 1, 1)
                invert_sums(b, 1)
                for q in range(QUARTERS):
                    if 0 < q < QUARTERS - 1:
                        weigh(b, q + 1, 0)
                        weigh(b, q + 1, 1)
                    if q + 1 < QUARTERS:
                        elu_out(b, q)
                        for h in range(HALF):
                            dve.wait_ge(elu_done[h], QUARTERS * b + q + 1)
                            mix_channels(b, j, q + 1, h)

            dve.wait_ge(const_in, 48)
            nc.vector.tensor_copy(ident_b[:, :], ident).then_inc(casts_done, 1)
            nc.vector.tensor_copy(mask_b[:, :], const[:, C_MASK:C_MASK + MASKS]).then_inc(casts_done, 1)
            part = vec[:, 0:8].rearrange("p (s n) -> p n s", s=2)
            chain(nc.vector.tensor_scalar(bn[:, 0, :], part[:, 3, :], 1e-5, None, ALU.add))
            nc.vector.tensor_scalar(mix[:, 0:1], vec[:, 8:9], -1.0, 1.0, ALU.mult, ALU.add)
            nc.vector.tensor_scalar(mix[:, 1:2], vec[:, 8:9], -1.0, None, ALU.mult).then_inc(bn_var, 1)
            dve.wait_ge(bn_root, 1)
            chain(nc.vector.reciprocal(bn[:, 2, :], bn[:, 1, :]))
            chain(nc.vector.tensor_tensor(bn[:, 3, :], bn[:, 0, :], bn[:, 2, :], ALU.mult))
            chain(nc.vector.tensor_tensor(bn[:, 4, :], bn[:, 1, :], bn[:, 3, :], ALU.add))
            chain(nc.vector.tensor_scalar(bn[:, 3, :], bn[:, 4, :], 0.5, None, ALU.mult))
            chain(nc.vector.reciprocal(bn[:, 5, :], bn[:, 3, :]))
            chain(nc.vector.tensor_tensor(bn[:, 6, :], part[:, 0, :], bn[:, 5, :], ALU.mult))
            chain(nc.vector.tensor_tensor(bn[:, 2, :], part[:, 2, :], bn[:, 6, :], ALU.mult))
            nc.vector.tensor_tensor(bn[:, 7, :], part[:, 1, :], bn[:, 2, :], ALU.subtract).then_inc(bn_done, 1)
            attend(0, True)
            with dve.Fori(0, B // BUFS) as k:
                for j in range(BUFS):
                    b = k * BUFS + j
                    finish(b, j, 32 * (k + 1))
                    attend(b + 1)
            finish(B - 1, (B - 1) % BUFS, 32 * ((B - 1) // BUFS + 1))
            elu_out(B - 1, QUARTERS - 1)

        @block.tensor
        def _(pe):
            def mm(o, l, r, start, stop, **kw):
                return nc.tensor.matmul(o, l, r, start=start, stop=stop, skip_group_check=True, **kw)

            def transpose_x(b, j, q, first):
                xb = xs[j]
                if q == QUARTERS - 1 and not first:
                    pe.wait_ge(pt_out, QUARTERS * b)
                for t in range(2):
                    g = 2 * q + t
                    if q > 0:
                        pe.wait_ge(xt_out, EVACS * b + g - 1)
                    elif not first and t == 0:
                        pe.wait_ge(exp_done, QUARTERS * b - 3)
                    for v in range(2):
                        for h in range(HALF):
                            at0 = (2 * g + v) * WIN
                            last = nc.tensor.transpose(xp[t][:, v * C + h * P:v * C + (h + 1) * P],
                                                       xb[:, h, at0:at0 + WIN], ident)
                    last.then_inc(xt_done, 1)
                    if g == EVACS - 3:
                        for h in range(HALF):
                            last = nc.tensor.transpose(et[0:64, h * P:(h + 1) * P],
                                                       xb[:, h, GROUPS * WIN:GROUPS * WIN + 64], ident)
                        last.then_inc(xt_done, 1)

            def gram_band(b, q, first):
                last_q = q == QUARTERS - 1
                pe.wait_ge(xt_out, EVACS * b + (EVACS if last_q else 2 * (q + 1)))
                if q == 0 and not first:
                    pe.wait_ge(gram_ready, b)
                for v in range(q * GQ, (q + 1) * GQ + last_q):
                    k = P if v < GROUPS else P // 2
                    for blk in range(P // HID):
                        mine, other = blk * HID, P + blk * HID - 1
                        last = mm(gb[mine:mine + HID, 0:BAND], upper[0:k, v, mine:mine + HID],
                                  upper[0:k, v, other:other + BAND], v == 0, v == GROUPS, tile_position=(0, mine))
                if last_q:
                    last.then_inc(gram_done, 1)

            def shift_gram(b):
                pe.wait_ge(gram_side, b + 1)
                mm(gb[:, SHIFT:SHIFT + 1], const[:, C_DOWN:C_DOWN + P], gram[:, 0:1], True, True)\
                    .then_inc(shift_done, 1)

            def project_query(b, j, first):
                xb = xs[j]
                if not first:
                    pe.wait_ge(hs_out, SUMS * b - 1)
                for h in range(HALF):
                    for q in range(QUARTERS):
                        last = mm(pj[q * HID:(q + 1) * HID, :], wt[:, h, 0:HID], xb[:, h, W + q * QN:W + (q + 1) * QN],
                                  h == 0, h == HALF - 1, tile_position=(0, q * HID))
                last.then_inc(proj_done, 1)

            def project_key(b, j, first):
                xb = xs[j]
                if not first:
                    pe.wait_ge(hs_out, SUMS * b)
                for h in range(HALF):
                    for q in range(QUARTERS):
                        last = mm(at[q * HID:(q + 1) * HID, :], wt[:, h, HID:], xb[:, h, W + q * QN:W + (q + 1) * QN],
                                  h == 0, h == HALF - 1, tile_position=(0, q * HID))
                last.then_inc(proj_done, 1)
                pe.wait_ge(proj_out, 3 * b + 1)
                for h in range(HALF):
                    rows = xb[:, h, :].rearrange("p (r w) -> p r w", w=W)
                    for q in range(QUARTERS):
                        last = mm(pj[q * HID:(q + 1) * HID, 0:2 * W], wt[:, h, HID:],
                                  rows[:, q * QR:q * QR + QR + 2:QR + 1, :],
                                  h == 0, h == HALF - 1, tile_position=(0, q * HID))
                last.then_inc(proj_done, 1)

            def scores(b, q, first):
                if q == 0:
                    pe.wait_ge(proj_out, 3 * b + 3)
                    pe.wait_ge(xt_out, EVACS * (b + 1))
                elif q > 1 and not first:
                    pe.wait_ge(elu_done[q - 2], QUARTERS * b)
                m0 = (q > 0) * WIN + (q == QUARTERS - 1) * WIN
                mm(score[q][:, :], ident_b[:, :], mask_b[:, m0:m0 + GQ * WIN], True, False)
                lo = q * HID
                for v in range(GQ):
                    for c in range(2):
                        last = mm(score[q][c * 64:(c + 1) * 64, v * WIN:(v + 1) * WIN],
                                  query[lo:lo + HID, v * WIN + c * NQ:v * WIN + (c + 1) * NQ],
                                  key[lo:lo + HID, v * WIN + c * 2 * W:v * WIN + c * 2 * W + WIN],
                                  False, True, tile_position=(lo, c * 64))
                last.then_inc(score_done, 1)

            def transpose_probs(b, q):
                pe.wait_ge(exp_done, QUARTERS * b + q + 1)
                if q > 0:
                    pe.wait_ge(pt_out, QUARTERS * b + q)
                else:
                    pe.wait_ge(xt_out, EVACS * (b + 1))
                for v in range(GQ):
                    last = nc.tensor.transpose(et[:, v * P:(v + 1) * P], probs[q % 2][:, v, :], ident)
                last.then_inc(pt_done, 1)

            def attend(b, j, first=False):
                project_key(b, j, first)
                gram_band(b, 3, first)
                scores(b, 0, first)
                if not first:
                    add_spatial(b - 1, QUARTERS - 1, 0)
                    add_spatial(b - 1, QUARTERS - 1, 1)
                scores(b, 1, first)
                shift_gram(b)
                transpose_probs(b, 0)
                scores(b, 2, first)
                scores(b, 3, first)
                transpose_probs(b, 1)

            def window_sums(b, q, t):
                pe.wait_ge(pt_out, QUARTERS * b + q + 1)
                if t == 0:
                    pe.wait_ge(lower_in[q], 32 * (b + 1))
                    if q + 1 < QUARTERS:
                        pe.wait_ge(lower_in[q + 1], 32 * (b + 1))
                if q > 0:
                    pe.wait_ge(hs_out, SUMS * b + PARTS * (q - 1) + t + 1)
                elif t == 1:
                    pe.wait_ge(exp_done, QUARTERS * b + 2)
                for i in range(GV):
                    v = t * GV + i
                    for c, window in enumerate((upper, lower)):
                        last = mm(part_bank[t][c * NQ:(c + 1) * NQ, i * C:(i + 1) * C],
                                  probs_t[:, q, v * P + c * NQ:v * P + (c + 1) * NQ],
                                  window[:, q * GQ + v, :], True, True, tile_position=(0, c * NQ))
                last.then_inc(hs_done, 1)

            def add_spatial(b, q, h):
                pe.wait_ge(channel_done, 2 * (QUARTERS * b + q) + h + 1)
                for t in range(PARTS):
                    pe.wait_ge(hs_out, SUMS * b + PARTS * q + t + 1)
                    for v in range(t * GV, (t + 1) * GV):
                        last = mm(z[h][:, v * P:(v + 1) * P], spatial[q % 2][:, v, h * P:(h + 1) * P], ident,
                                  False, v == GQ - 1, is_transpose=True)
                last.then_inc(z_done, 1)

            def finish(b, n=None, n_loaded=None):
                window_sums(b, 0, 0)
                window_sums(b, 0, 1)
                transpose_probs(b, 2)
                window_sums(b, 1, 0)
                transpose_probs(b, 3)
                window_sums(b, 1, 1)
                for q in range(QUARTERS):
                    if 0 < q < QUARTERS - 1:
                        window_sums(b, q + 1, 0)
                        window_sums(b, q + 1, 1)
                    if q + 1 < QUARTERS or n is None:
                        add_spatial(b, q, 0)
                        add_spatial(b, q, 1)
                    if n is not None:
                        if q == 0:
                            pe.wait_ge(x_in[n], n_loaded)
                        if q == QUARTERS - 1:
                            project_query(b + 1, n, False)
                        transpose_x(b + 1, n, q, False)
                        if q > 0:
                            gram_band(b + 1, q - 1, False)

            pe.wait_ge(const_in, 48)
            pe.wait_ge(casts_done, 2)
            for q in range(QUARTERS):
                pe.wait_ge(first_in[q], 16)
                transpose_x(0, 0, q, True)
                if q > 0:
                    gram_band(0, q - 1, True)
            project_query(0, 0, True)
            attend(0, 0, True)
            with pe.Fori(0, B // BUFS) as k:
                for j in range(BUFS):
                    b = k * BUFS + j
                    n = (j + 1) % BUFS
                    finish(b, n, 16 * (k + 1 + (j + 1) // BUFS))
                    attend(b + 1, n)
            finish(B - 1)


def shape_constants():
    import numpy as np
    const = np.zeros((P, C_ALL), np.float32)
    i = np.arange(P)
    const[i, C_ID + i] = 1.0
    const[i[1:], C_DOWN + i[:-1]] = 1.0
    const[i, C_BAND + i % HID] = 1.0
    const[0, C_BAND] = 0.0
    for n in range(1, 3):
        const[i, C_BAND + n * BAND + i % HID + 1] = 1.0
    const[0, C_END] = NEG
    const[P - 1, C_END + 3] = NEG
    kind, query_row, query_col = i // NQ, (i // W) % 2 + 1, i % W
    key_row, key_col = np.arange(WIN) // W, np.arange(WIN) % W
    di = abs(query_row[:, None] - key_row)
    dj = abs(query_col[:, None] - key_col)
    near = (di <= 1) & (dj <= 1) & ~((di == 0) & (dj == 0))
    for n in range(6):
        inside = np.ones((P, WIN), bool)
        if n == 0:
            inside &= ~((kind[:, None] == 0) & (key_row == 0))
        if n == 5:
            inside &= ~((kind[:, None] == 1) & (key_row == WR - 1))
        const[:, C_MASK + n * WIN:C_MASK + (n + 1) * WIN] = np.where(near & inside, 0.0, NEG)
    return const


def kernel(**inputs):
    import numpy as np
    import concourse.bacc as bacc
    from concourse.bass_utils import run_bass_kernel_spmd

    a = {name.replace("L0_conv_", ""): np.asarray(v) for name, v in inputs.items()}
    w_t = np.concatenate([a["wa"], a["ws"]], axis=0).T.reshape(P, HALF, 2 * HID)
    norms = np.stack([a[n + s] for s in "as" for n in "gbmv"], axis=1)
    vectors = np.concatenate([np.tile(norms, (QUARTERS, 1)), np.tile(a["gama"].reshape(1, 1), (P, 1))], axis=1)
    arrays = {"x_dram": a["x"], "w_dram": w_t, "vectors_dram": vectors, "constants_dram": shape_constants()}
    arrays = {name: np.ascontiguousarray(v) for name, v in arrays.items()}

    nc = bacc.Bacc("TRN2", target_bir_lowering=False, num_devices=1)
    args = [nc.dram_tensor(name, v.shape, mybir.dt.from_np(v.dtype), kind="ExternalInput").ap()
            for name, v in arrays.items()]
    out = nc.dram_tensor("out_dram", (B, C, H, W), mybir.dt.float32, kind="ExternalOutput").ap()
    graph_attention(nc, *args, out)
    result = run_bass_kernel_spmd(nc, [arrays], core_ids=[0])
    return result.results[0]["out_dram"]
```
